# Optimizing a Trainium2 kernel written in Bass

```python
import numpy as np
import jax
import jax.numpy as jnp

def _softmax(x, axis=-1):
    return jax.nn.softmax(x, axis=axis)

def _gelu(x):
    return jax.nn.gelu(x, approximate=True)

def _silu(x):
    return jax.nn.silu(x)

def _sigmoid(x):
    return jax.nn.sigmoid(x)

def _layernorm(x, axis=-1, eps=1e-05):
    m = jnp.mean(x, axis=axis, keepdims=True)
    v = jnp.var(x, axis=axis, keepdims=True)
    return (x - m) / jnp.sqrt(v + eps)

def _scatter_add(tgt, idx, src, axis=0):
    return tgt.at[idx].add(src)

def _segment_sum(src, seg, n):
    return jax.ops.segment_sum(src, seg, n)
kernel_name = 'mk_prb_d1_jaxref_r8_16d3a0'

def setup_inputs(seed: int=0):
    np.random.seed(seed)
    _w = jnp.asarray

    def _L0_attn_setup():
        import jax, jax.numpy as jnp
        import numpy as np
        EPS = 1e-06

        def _rmsnorm(x, w):
            x32 = x.astype(jnp.float32)
            n = x32 * jax.lax.rsqrt(jnp.mean(x32 * x32, axis=-1, keepdims=True) + EPS)
            return n.astype(x.dtype) * w

        def _reference_tuple_inner(u, dt, A, Bmat, C, D, norm_w):
            u = _rmsnorm(u, norm_w)
            Bsz, T, _ = u.shape
            dts = jax.nn.sigmoid(dt)
            a = jnp.exp(-dts * jnp.abs(A))
            t = jnp.arange(T, dtype=jnp.float32)
            h = dts[:, None] * a[:, None] ** t[None, :]
            u_proj = jnp.einsum('bti,is->bst', u, Bmat)
            k = jnp.flip(h, axis=1)[:, None, :]
            x = jax.lax.conv_general_dilated(u_proj, k, window_strides=(1,), padding=[(T - 1, T - 1)], dimension_numbers=('NCW', 'OIW', 'NCW'), feature_group_count=u_proj.shape[1])[:, :, :T]
            x = jnp.transpose(x, (0, 2, 1))
            y = jnp.einsum('bts,so->bto', x, C) + D
            return (y, x[:, -1])
        key = jax.random.key(seed)
        ks = jax.random.split(key, 8)
        I, S, O = (128, 64, 128)
        Bsz, T = (4, 256)
        return {'u': jax.random.normal(ks[0], (Bsz, T, I), dtype=jnp.float32), 'dt': jax.random.normal(ks[1], (S,), dtype=jnp.float32), 'A': jax.random.normal(ks[2], (S,), dtype=jnp.float32), 'Bmat': jax.random.normal(ks[3], (I, S), dtype=jnp.float32) / np.sqrt(S), 'C': jax.random.normal(ks[4], (S, O), dtype=jnp.float32) / np.sqrt(S), 'D': jax.random.normal(ks[5], (O,), dtype=jnp.float32), 'norm_w': jnp.ones((I,), dtype=jnp.float32)}
    _L0_attn_in = _L0_attn_setup()

    def _L0_ffn_setup():
        import jax, jax.numpy as jnp
        import numpy as np
        DIM = 128
        DEPTH = 2
        HEADS = 8
        DIM_HEAD = 64
        WINDOW = 64
        INNER = HEADS * DIM_HEAD
        HID = int(DIM * 4 * 2 / 3)
        B, N = (2, 1024)
        QK_SCALE = 8.0

        def shift_token(t):
            t1, t2 = jnp.split(t, 2, axis=-1)
            t2 = jnp.pad(t2, ((0, 0), (1, 0), (0, 0)))[:, :-1]
            return jnp.concatenate([t1, t2], axis=-1)

        def l2norm(t):
            return t / jnp.clip(jnp.linalg.norm(t, axis=-1, keepdims=True), 1e-12)

        def rotate_half(x):
            x1, x2 = jnp.split(x, 2, axis=-1)
            return jnp.concatenate([-x2, x1], axis=-1)

        def rotary_xpos(q, k):
            n = q.shape[-2]
            half_idx = jnp.arange(0, DIM_HEAD, 2, dtype=jnp.float32)
            inv_freq = 1.0 / 10000.0 ** (half_idx / DIM_HEAD)
            t = jnp.arange(n, dtype=jnp.float32)
            freqs = t[:, None] * inv_freq[None, :]
            freqs = jnp.concatenate([freqs, freqs], axis=-1)
            base = (half_idx + 0.4 * DIM_HEAD) / (1.4 * DIM_HEAD)
            power = (t - n // 2) / float(WINDOW // 2)
            scale = base[None, :] ** power[:, None]
            scale = jnp.concatenate([scale, scale], axis=-1)
            cos, sin = (jnp.cos(freqs), jnp.sin(freqs))
            q = q * cos * scale + rotate_half(q) * sin * scale
            k = k * cos / scale + rotate_half(k) * sin / scale
            return (q, k)

        def local_attention(q, k, v):
            b, h, n, d = q.shape
            w = n // WINDOW
            bq = q.reshape(b, h, w, WINDOW, d) * QK_SCALE
            bk = k.reshape(b, h, w, WINDOW, d)
            bv = v.reshape(b, h, w, WINDOW, d)

            def look_around(t):
                p = jnp.pad(t, ((0, 0), (0, 0), (1, 0), (0, 0), (0, 0)))
                return jnp.concatenate([p[:, :, :w], p[:, :, 1:]], axis=3)
            bk, bv = (look_around(bk), look_around(bv))
            bt = jnp.arange(n).reshape(w, WINDOW)
            btp = jnp.pad(bt, ((1, 0), (0, 0)), constant_values=-1)
            btk = jnp.concatenate([btp[:w], btp[1:]], axis=1)
            sim = jnp.einsum('bhwid,bhwjd->bhwij', bq, bk)
            i = bt[:, :, None]
            j = btk[:, None, :]
            mask = (i < j) | (i > j + WINDOW) | (j == -1)
            sim = jnp.where(mask, -jnp.finfo(sim.dtype).max, sim)
            attn = jax.nn.softmax(sim, axis=-1)
            out = jnp.einsum('bhwij,bhwjd->bhwid', attn, bv)
            return out.reshape(b, h, n, d)

        def _layer(x, wqkv, qs, ksc, wo, lg, lb, w1, b1, w2, b2):
            b, n, _ = x.shape
            h = shift_token(x)
            qkv = h @ wqkv
            q, k, v = jnp.split(qkv, 3, axis=-1)
            to_heads = lambda t: t.reshape(b, n, HEADS, DIM_HEAD).transpose(0, 2, 1, 3)
            q, k, v = (to_heads(q), to_heads(k), to_heads(v))
            q = l2norm(q) * qs
            k = l2norm(k) * ksc
            q, k = rotary_xpos(q, k)
            o = local_attention(q, k, v)
            o = o.transpose(0, 2, 1, 3).reshape(b, n, INNER)
            x = x + o @ wo
            h = shift_token(x)
            mu = h.mean(-1, keepdims=True)
            var = h.var(-1, keepdims=True)
            h = (h - mu) / jnp.sqrt(var + 1e-05) * lg + lb
            h = h @ w1 + b1
            a, g = jnp.split(h, 2, axis=-1)
            h = a * jax.nn.gelu(g, approximate=False)
            x = x + h @ w2 + b2
            return x
        key = jax.random.key(seed)
        ks = jax.random.split(key, 6)
        return {'x': jax.random.normal(ks[0], (B, N, DIM), jnp.float32), 'wqkv': jax.random.normal(ks[1], (DEPTH, DIM, 3 * INNER), jnp.float32) * 0.02, 'q_scale': jnp.ones((DEPTH, DIM_HEAD), jnp.float32), 'k_scale': jnp.ones((DEPTH, DIM_HEAD), jnp.float32), 'wo': jax.random.normal(ks[2], (DEPTH, INNER, DIM), jnp.float32) * 0.02, 'ln_g': jnp.ones((DEPTH, DIM), jnp.float32), 'ln_b': jnp.zeros((DEPTH, DIM), jnp.float32), 'w1': jax.random.normal(ks[3], (DEPTH, DIM, 2 * HID), jnp.float32) * 0.02, 'b1': jnp.zeros((DEPTH, 2 * HID), jnp.float32), 'w2': jax.random.normal(ks[4], (DEPTH, HID, DIM), jnp.float32) * 0.02, 'b2': jnp.zeros((DEPTH, DIM), jnp.float32)}
    _L0_ffn_in = _L0_ffn_setup()
    _d = {'L0_attn_u': _L0_attn_in['u'], 'L0_attn_dt': _L0_attn_in['dt'], 'L0_attn_A': _L0_attn_in['A'], 'L0_attn_Bmat': _L0_attn_in['Bmat'], 'L0_attn_C': _L0_attn_in['C'], 'L0_attn_D': _L0_attn_in['D'], 'L0_attn_norm_w': _L0_attn_in['norm_w'], 'L0_ffn_wqkv': _L0_ffn_in['wqkv'], 'L0_ffn_q_scale': _L0_ffn_in['q_scale'], 'L0_ffn_k_scale': _L0_ffn_in['k_scale'], 'L0_ffn_wo': _L0_ffn_in['wo'], 'L0_ffn_ln_g': _L0_ffn_in['ln_g'], 'L0_ffn_ln_b': _L0_ffn_in['ln_b'], 'L0_ffn_w1': _L0_ffn_in['w1'], 'L0_ffn_b1': _L0_ffn_in['b1'], 'L0_ffn_w2': _L0_ffn_in['w2'], 'L0_ffn_b2': _L0_ffn_in['b2']}
    _x0 = _d['L0_attn_u']
    _d['L0_attn_u'] = jax.random.normal(jax.random.fold_in(jax.random.key(seed), 1), (16, 512, 128), dtype=_x0.dtype)
    del _x0
    return _d

def reference(L0_attn_u, L0_attn_dt, L0_attn_A, L0_attn_Bmat, L0_attn_C, L0_attn_D, L0_attn_norm_w, L0_ffn_wqkv, L0_ffn_q_scale, L0_ffn_k_scale, L0_ffn_wo, L0_ffn_ln_g, L0_ffn_ln_b, L0_ffn_w1, L0_ffn_b1, L0_ffn_w2, L0_ffn_b2):

    def _L0_attn_ref(u, dt, A, Bmat, C, D, norm_w):
        import jax, jax.numpy as jnp
        import numpy as np
        EPS = 1e-06

        def _rmsnorm(x, w):
            x32 = x.astype(jnp.float32)
            n = x32 * jax.lax.rsqrt(jnp.mean(x32 * x32, axis=-1, keepdims=True) + EPS)
            return n.astype(x.dtype) * w

        def _reference_tuple_inner(u, dt, A, Bmat, C, D, norm_w):
            u = _rmsnorm(u, norm_w)
            Bsz, T, _ = u.shape
            dts = jax.nn.sigmoid(dt)
            a = jnp.exp(-dts * jnp.abs(A))
            t = jnp.arange(T, dtype=jnp.float32)
            h = dts[:, None] * a[:, None] ** t[None, :]
            u_proj = jnp.einsum('bti,is->bst', u, Bmat)
            k = jnp.flip(h, axis=1)[:, None, :]
            x = jax.lax.conv_general_dilated(u_proj, k, window_strides=(1,), padding=[(T - 1, T - 1)], dimension_numbers=('NCW', 'OIW', 'NCW'), feature_group_count=u_proj.shape[1])[:, :, :T]
            x = jnp.transpose(x, (0, 2, 1))
            y = jnp.einsum('bts,so->bto', x, C) + D
            return (y, x[:, -1])
        return _reference_tuple_inner(u, dt, A, Bmat, C, D, norm_w)[0]

    def _L0_ffn_ref(x, wqkv, q_scale, k_scale, wo, ln_g, ln_b, w1, b1, w2, b2):
        import jax, jax.numpy as jnp
        import numpy as np
        DIM = 128
        DEPTH = 2
        HEADS = 8
        DIM_HEAD = 64
        WINDOW = 64
        INNER = HEADS * DIM_HEAD
        HID = int(DIM * 4 * 2 / 3)
        B, N = (2, 1024)
        QK_SCALE = 8.0

        def shift_token(t):
            t1, t2 = jnp.split(t, 2, axis=-1)
            t2 = jnp.pad(t2, ((0, 0), (1, 0), (0, 0)))[:, :-1]
            return jnp.concatenate([t1, t2], axis=-1)

        def l2norm(t):
            return t / jnp.clip(jnp.linalg.norm(t, axis=-1, keepdims=True), 1e-12)

        def rotate_half(x):
            x1, x2 = jnp.split(x, 2, axis=-1)
            return jnp.concatenate([-x2, x1], axis=-1)

        def rotary_xpos(q, k):
            n = q.shape[-2]
            half_idx = jnp.arange(0, DIM_HEAD, 2, dtype=jnp.float32)
            inv_freq = 1.0 / 10000.0 ** (half_idx / DIM_HEAD)
            t = jnp.arange(n, dtype=jnp.float32)
            freqs = t[:, None] * inv_freq[None, :]
            freqs = jnp.concatenate([freqs, freqs], axis=-1)
            base = (half_idx + 0.4 * DIM_HEAD) / (1.4 * DIM_HEAD)
            power = (t - n // 2) / float(WINDOW // 2)
            scale = base[None, :] ** power[:, None]
            scale = jnp.concatenate([scale, scale], axis=-1)
            cos, sin = (jnp.cos(freqs), jnp.sin(freqs))
            q = q * cos * scale + rotate_half(q) * sin * scale
            k = k * cos / scale + rotate_half(k) * sin / scale
            return (q, k)

        def local_attention(q, k, v):
            b, h, n, d = q.shape
            w = n // WINDOW
            bq = q.reshape(b, h, w, WINDOW, d) * QK_SCALE
            bk = k.reshape(b, h, w, WINDOW, d)
            bv = v.reshape(b, h, w, WINDOW, d)

            def look_around(t):
                p = jnp.pad(t, ((0, 0), (0, 0), (1, 0), (0, 0), (0, 0)))
                return jnp.concatenate([p[:, :, :w], p[:, :, 1:]], axis=3)
            bk, bv = (look_around(bk), look_around(bv))
            bt = jnp.arange(n).reshape(w, WINDOW)
            btp = jnp.pad(bt, ((1, 0), (0, 0)), constant_values=-1)
            btk = jnp.concatenate([btp[:w], btp[1:]], axis=1)
            sim = jnp.einsum('bhwid,bhwjd->bhwij', bq, bk)
            i = bt[:, :, None]
            j = btk[:, None, :]
            mask = (i < j) | (i > j + WINDOW) | (j == -1)
            sim = jnp.where(mask, -jnp.finfo(sim.dtype).max, sim)
            attn = jax.nn.softmax(sim, axis=-1)
            out = jnp.einsum('bhwij,bhwjd->bhwid', attn, bv)
            return out.reshape(b, h, n, d)

        def _layer(x, wqkv, qs, ksc, wo, lg, lb, w1, b1, w2, b2):
            b, n, _ = x.shape
            h = shift_token(x)
            qkv = h @ wqkv
            q, k, v = jnp.split(qkv, 3, axis=-1)
            to_heads = lambda t: t.reshape(b, n, HEADS, DIM_HEAD).transpose(0, 2, 1, 3)
            q, k, v = (to_heads(q), to_heads(k), to_heads(v))
            q = l2norm(q) * qs
            k = l2norm(k) * ksc
            q, k = rotary_xpos(q, k)
            o = local_attention(q, k, v)
            o = o.transpose(0, 2, 1, 3).reshape(b, n, INNER)
            x = x + o @ wo
            h = shift_token(x)
            mu = h.mean(-1, keepdims=True)
            var = h.var(-1, keepdims=True)
            h = (h - mu) / jnp.sqrt(var + 1e-05) * lg + lb
            h = h @ w1 + b1
            a, g = jnp.split(h, 2, axis=-1)
            h = a * jax.nn.gelu(g, approximate=False)
            x = x + h @ w2 + b2
            return x
        for l in range(DEPTH):
            x = _layer(x, wqkv[l], q_scale[l], k_scale[l], wo[l], ln_g[l], ln_b[l], w1[l], b1[l], w2[l], b2[l])
        return x
    x = L0_attn_u
    xn = _layernorm(x, axis=-1)
    x = x + _L0_attn_ref(xn, L0_attn_dt, L0_attn_A, L0_attn_Bmat, L0_attn_C, L0_attn_D, L0_attn_norm_w) + _L0_ffn_ref(xn, L0_ffn_wqkv, L0_ffn_q_scale, L0_ffn_k_scale, L0_ffn_wo, L0_ffn_ln_g, L0_ffn_ln_b, L0_ffn_w1, L0_ffn_b1, L0_ffn_w2, L0_ffn_b2)
    return x

_drawn_inputs = setup_inputs


def setup_inputs(seed=0):
    import zlib

    import numpy as np

    out = dict(_drawn_inputs(seed))
    spreads = {'L0_attn_norm_w': (1.0, 0.6),
     'L0_ffn_q_scale': (1.0, 0.6),
     'L0_ffn_k_scale': (1.0, 0.6),
     'L0_ffn_ln_g': (1.0, 0.6),
     'L0_ffn_ln_b': (0.0, 0.8),
     'L0_ffn_b1': (0.0, 0.8),
     'L0_ffn_b2': (0.0, 0.779)}
    factors = {'L0_ffn_wqkv': 5.07,
     'L0_ffn_wo': 5.07,
     'L0_ffn_w1': 8.0,
     'L0_ffn_w2': 8.0,
     'L0_attn_dt': 2.92}
    for name, (base, spread) in spreads.items():
        noise = np.random.default_rng([zlib.crc32(name.encode()), seed]).standard_normal(out[name].shape)
        drawn = base * np.exp(spread * noise) if base else spread * noise
        out[name] = jnp.asarray(drawn.astype(out[name].dtype))
    for name, factor in factors.items():
        out[name] = (out[name] * factor).astype(out[name].dtype)
    return out
```

```python
from contextlib import ExitStack

import numpy as np

import concourse.bass as bass
from concourse import mybir

F32 = mybir.dt.float32
F32R = mybir.dt.float32r
BF16 = mybir.dt.bfloat16
ALU = mybir.AluOpType
ACT = mybir.ActivationFunctionType
AX = mybir.AxisListType

P = 128
NB = 16
SEQ = 512
D = 128
TILES = SEQ // P
HEADS = 8
PAIRS = HEADS // 2
DH = 64
WIN = 64
INNER = HEADS * DH
HID = D * 4 * 2 // 3
LAYERS = 2
S = 64
HB = 3
HM = -(-HID // HB)
HROWS = [min(HM, HID - HM * j) for j in range(HB)]
QK_SCALE = 8.0
MASKED = -1e30
STEPS = LAYERS * NB


def rotary_tables():
    half = np.arange(0, DH, 2, dtype=np.float32)
    inv_freq = (np.float32(1.0) / np.float32(10000.0) ** (half / np.float32(DH))).astype(np.float32)
    t = np.arange(SEQ, dtype=np.float32)
    freqs = t[:, None] * inv_freq[None, :]
    base = (half + np.float32(0.4 * DH)) / np.float32(1.4 * DH)
    power = (t - SEQ // 2) / np.float32(WIN // 2)
    scale = (base[None, :] ** power[:, None]).astype(np.float32)
    cos, sin = np.cos(freqs), np.sin(freqs)
    both = lambda a, b: np.concatenate([a, b], axis=-1)
    c = np.stack([both(cos * scale, cos * scale), both(cos / scale, cos / scale)], 1)
    s = np.stack([both(-sin * scale, sin * scale), both(-sin / scale, sin / scale)], 1)
    lay = lambda a: np.ascontiguousarray(
        a.astype(np.float32).reshape(TILES, P, 2, DH).transpose(1, 0, 2, 3))
    return lay(c), lay(s)


def masks():
    r, c = np.arange(P)[:, None], np.arange(P + WIN)[None, :]
    seen = (r <= c) & (c <= r + WIN)
    q_mask = np.stack([seen & (c >= WIN), seen], 1)
    k, q = np.arange(WIN)[:, None], np.arange(WIN)[None, :]
    own, before, none = k <= q, k >= q, np.zeros((WIN, WIN), bool)
    first = np.concatenate([np.concatenate([own, before], 1), np.concatenate([none, own], 1)], 0)
    later = np.concatenate([np.concatenate([own, before], 1), np.concatenate([before, own], 1)], 0)
    k_mask = np.stack([first, later], 1)
    add = lambda m: np.where(m, np.float32(0), np.float32(MASKED)).astype(np.float32)
    return add(q_mask), add(k_mask)


def selectors():
    sel = np.zeros((2 * HEADS, HEADS, P), np.float32)
    for h in range(HEADS):
        row = 4 * (h % 2) + h // 2
        sel[row, h] = sel[HEADS + row, h] = -1.0
    return sel


def wait(eng, sem, value):
    if not (isinstance(value, int) and value <= 0):
        eng.wait_ge(sem, value)


def build(nc, i, out, acc_dram):
    u_tok = i["u"].rearrange("b (t p) d -> b p t d", p=P)
    out_tok = out.rearrange("b (t p) d -> b p t d", p=P)
    acc_tok = acc_dram.rearrange("b (t p) d -> b p t d", p=P)

    with ExitStack() as ctx:
        def sb(name, shape, dt=F32):
            return ctx.enter_context(nc.sbuf_tensor(name, shape, dt))

        w = {
            "ident": sb("ident", [P, P]),
            "ident_b": sb("ident_b", [P, P], BF16),
            "q_mask": sb("q_mask", [P, 2, P + WIN], BF16),
            "k_mask": sb("k_mask", [P, 2, P], BF16),
            "sel": sb("sel", [2 * HEADS, HEADS, P], BF16),
            "minus_half": sb("minus_half", [P, 16]),
            "cos": sb("cos", [P, LAYERS, TILES, 2, DH]),
            "sin": sb("sin", [P, LAYERS, TILES, 2, DH]),
            "wqkv_hi": sb("wqkv_hi", [P, LAYERS, 3 * INNER], F32R),
            "wqkv_lo": sb("wqkv_lo", [P, LAYERS, 3 * INNER], F32R),
            "w1_hi": sb("w1_hi", [P, LAYERS, 2 * HID], F32R),
            "w1_lo": sb("w1_lo", [P, LAYERS, 2 * HID], F32R),
            "wo": sb("wo", [P, LAYERS, PAIRS, D]),
            "w2": sb("w2", [HM, LAYERS, HB, D]),
            "b1": sb("b1", [HM, LAYERS, 2 * HB]),
            "b2": sb("b2", [P, LAYERS]),
            "xT": sb("xT", [P, NB * SEQ]),
        }
        with ExitStack() as first:
            first_pass(nc, first, i, u_tok, acc_tok, w)
        with ExitStack() as layers:
            layer_steps(nc, layers, acc_tok, out_tok, w)


def first_pass(nc, ctx, i, u_tok, acc_tok, w):
    def sb(name, shape, dt=F32):
        return ctx.enter_context(nc.sbuf_tensor(name, shape, dt))

    def pb(name, shape, dt=F32):
        return ctx.enter_context(nc.psum_tensor(name, shape, dt))

    def sem(name):
        return ctx.enter_context(nc.semaphore(name))

    wqkv_raw = sb("wqkv_raw", [P, LAYERS, 3 * INNER])
    w1_raw = sb("w1_raw", [P, LAYERS, 2 * HID])
    w1_scaled = sb("w1_scaled", [P, LAYERS, 2 * HID])
    q_mask_raw = sb("q_mask_raw", [P, 2, P + WIN])
    k_mask_raw = sb("k_mask_raw", [P, 2, P])
    sel_raw = sb("sel_raw", [2 * HEADS, HEADS, P])
    rot_raw = sb("rot_raw", [P, 2, TILES, 2, DH])
    scales = sb("scales", [P, LAYERS, 2, DH])
    b1_raw = sb("b1_raw", [HM, LAYERS, 2 * HB])
    ln_g = sb("ln_g", [P, LAYERS])
    ln_b = sb("ln_b", [P, LAYERS])
    b_raw = sb("b_raw", [P, S])
    b_mat = sb("b_mat", [P, S])
    norm_w = sb("norm_w", [P, 1])
    c_mat = sb("c_mat", [S, D])
    d_row = sb("d_row", [1, D])
    ones_row = sb("ones_row", [1, P])
    dt_a = sb("dt_a", [S, 2])
    col = sb("col", [S, 24])
    decay = sb("decay", [S, SEQ])

    u = sb("u", [P, 2, TILES, D])
    stats = sb("stats", [P, 2, TILES, 6])
    mv = sb("mv", [P, 2, TILES, 2])
    var_eps = sb("var_eps", [P, 2, TILES])
    rstd = sb("rstd", [P, 2, TILES])
    xn = sb("xn", [P, 2, TILES, D])
    dump = sb("dump", [P, D])
    spare = sb("spare", [P, 1])
    sums = sb("sums", [P, 2, TILES])
    sums_eps = sb("sums_eps", [P, 2, TILES])
    rms = sb("rms", [P, 2, TILES])
    un = sb("un", [P, 2, TILES, D])
    unT = sb("unT", [P, 2, SEQ])
    drive = sb("drive", [S, 2, SEQ])
    states = sb("states", [S, 2, SEQ])
    acc = sb("acc_first", [P, 2, TILES, D])

    p_x = [pb(f"p_x{h}", [P, SEQ]) for h in range(2)]
    p_u = [pb(f"p_u{h}", [P, SEQ]) for h in range(2)]
    p_proj = [pb(f"p_proj{h}", [P, SEQ]) for h in range(2)]
    p_y = [pb(f"p_y{h}", [P, SEQ]) for h in range(2)]

    early_in, late_in, weight_in, u_in = sem("early_in"), sem("late_in"), sem("weight_in"), [sem(f"u_in{h}") for h in range(2)]
    set_up, col_done, sigm, expd, b_ready = sem("set_up"), sem("col_done"), sem("sigm"), sem("expd"), sem("b_ready")
    hi_split, lo_split, w1_ready, folded = sem("hi_split"), sem("lo_split"), sem("w1_ready"), sem("folded")
    u_stat, u_mv, u_var, u_rstd = sem("u_stat"), sem("u_mv"), sem("u_var"), sem("u_rstd")
    xn_ready, sums_ready, sums_var, rms_ready = sem("xn_ready"), sem("sums_ready"), sem("sums_var"), sem("rms_ready")
    un_ready, xn_turned, un_turned = sem("un_ready"), sem("xn_turned"), sem("un_turned")
    x_copied, un_copied, projected, driven = sem("x_copied"), sem("un_copied"), sem("projected"), sem("driven")
    scanned, y_done, acc_ready, acc_out = sem("scanned"), sem("y_done"), sem("acc_ready"), [sem(f"acc_out{h}") for h in range(2)]
    square_done = sem("square_done")

    early = []
    late = []
    vec = lambda a: a.rearrange("(a b) -> a b", b=1)
    early += [(w["ident"][:, :], i["ident"]), (dt_a[:, 0:1], vec(i["dt"])), (dt_a[:, 1:2], vec(i["A"])),
              (b_raw[:, :], i["Bmat"]), (norm_w[:, :], vec(i["norm_w"])), (c_mat[:, :], i["C"]),
              (d_row[:, :], i["D"].rearrange("(a b) -> a b", a=1))]
    late += [(rot_raw[:, 0], i["rot_cos"]), (rot_raw[:, 1], i["rot_sin"]),
             (q_mask_raw[:, :, :], i["q_mask"]), (k_mask_raw[:, :, :], i["k_mask"]), (sel_raw[:, :, :], i["sel"])]
    for l in range(LAYERS):
        late += [(scales[:, l, 0, :], i["q_scale"][l:l + 1, :].partition_broadcast(P)),
                 (scales[:, l, 1, :], i["k_scale"][l:l + 1, :].partition_broadcast(P)),
                 (ln_g[:, l:l + 1], vec(i["ln_g"][l])), (ln_b[:, l:l + 1], vec(i["ln_b"][l])),
                 (w["b2"][:, l:l + 1], vec(i["b2"][l])),
                 (w["wo"][:, l], i["wo"][l].rearrange("(c p) d -> p c d", p=P)),
                 (wqkv_raw[:, l], i["wqkv"][l]), (w1_raw[:, l], i["w1"][l])]
        for j in range(HB):
            late.append((w["w2"][0:HROWS[j], l, j], i["w2"][l, HM * j:HM * j + HROWS[j], :]))
            for a in range(2):
                at = a * HID + HM * j
                late.append((b1_raw[0:HROWS[j], l, HB * a + j:HB * a + j + 1], vec(i["b1"][l, at:at + HROWS[j]])))

    def pairs(eng, step):
        for half in range(2):
            step(half, half, 0)
        with eng.Fori(1, NB // 2) as p:
            for half in range(2):
                step(2 * p + half, half, p)

    block = ctx.enter_context(nc.Block())

    @block.sync
    def _(sp):
        sp.dma_start(u[:, 0], u_tok[0]).then_inc(u_in[0], 16)
        for dst, src in early:
            sp.dma_start(dst, src).then_inc(early_in, 16)
        sp.dma_start(u[:, 1], u_tok[1]).then_inc(u_in[1], 16)
        for dst, src in late:
            sp.dma_start(dst, src).then_inc(late_in, 16)
        with sp.Fori(1, NB // 2) as p:
            for half in range(2):
                sp.wait_ge(acc_ready, 2 * p + (half - 1))
                sp.dma_start(u[:, half], u_tok[2 * p + half]).then_inc(u_in[half], 16)

    @block.gpsimd
    def _(pool):
        pool.memset(w["minus_half"][:, :], -0.5).then_inc(set_up, 1)
        pool.memset(ones_row[:, :], 1.0).then_inc(set_up, 1)
        pool.wait_ge(set_up, 2)

        def step(b, half, p):
            pool.wait_ge(u_var, b + 1)
            nc.gpsimd.tensor_tensor(rstd[:, half], var_eps[:, half], w["minus_half"][:, 0:TILES],
                                    ALU.pow).then_inc(u_rstd, 1)
            pool.wait_ge(sums_var, b + 1)
            nc.gpsimd.tensor_tensor(rms[:, half], sums_eps[:, half], w["minus_half"][:, 0:TILES],
                                    ALU.pow).then_inc(rms_ready, 1)

        pairs(pool, step)

    @block.vector
    def _(dve):
        count = [0]

        def chained(instruction):
            instruction.then_inc(col_done, 1)
            count[0] += 1
            dve.wait_ge(col_done, count[0])

        dve.wait_ge(early_in, 16 * len(early))
        nc.vector.tensor_scalar(b_mat[:, :], b_raw[:, :], norm_w[:, 0:1], None, ALU.mult).then_inc(b_ready, 1)
        dve.wait_ge(sigm, 1)
        chained(nc.vector.tensor_scalar(col[:, 1:2], col[:, 0:1], 1.0, None, ALU.add))
        chained(nc.vector.reciprocal(col[:, 2:3], col[:, 1:2]))
        chained(nc.vector.tensor_scalar(col[:, 3:4], dt_a[:, 1:2], -1.0, None, ALU.mult))
        chained(nc.vector.tensor_tensor(col[:, 4:5], col[:, 3:4], dt_a[:, 1:2], ALU.min))
        chained(nc.vector.tensor_tensor(col[:, 5:6], col[:, 4:5], col[:, 2:3], ALU.mult))
        chained(nc.vector.tensor_scalar(col[:, 6:7], col[:, 5:6], -0.35, None, ALU.max))
        chained(nc.vector.memset(col[:, 8:9], 1.0 / 9))
        for order in range(8, -1, -1):
            at = 8 + (9 - order)
            chained(nc.vector.tensor_scalar(col[:, at:at + 1], col[:, at - 1:at], col[:, 6:7], 1.0, ALU.mult, ALU.add))
            if order > 1:
                chained(nc.vector.tensor_scalar(col[:, 8 + (9 - order):9 + (9 - order)],
                                                col[:, 8 + (9 - order):9 + (9 - order)], 1.0 / order, None, ALU.mult))
        chained(nc.vector.tensor_scalar(col[:, 18:19], col[:, 5:6], -0.35, None, ALU.is_gt))
        dve.wait_ge(expd, 1)
        chained(nc.vector.tensor_tensor(col[:, 19:20], col[:, 17:18], col[:, 7:8], ALU.subtract))
        chained(nc.vector.tensor_tensor(col[:, 20:21], col[:, 19:20], col[:, 18:19], ALU.mult))
        chained(nc.vector.tensor_tensor(col[:, 21:22], col[:, 20:21], col[:, 7:8], ALU.add))
        chained(nc.vector.memset(decay[:, :], 1.0))
        chained(nc.vector.tensor_scalar(decay[:, :], decay[:, :], col[:, 21:22], None, ALU.mult))

        def step(b, half, p):
            dve.wait_ge(u_in[half], 16 * p + 16)
            for t in range(TILES):
                last = nc.vector.bn_stats(stats[:, half, t], u[:, half, t])
            last.then_inc(u_stat, 1)
            dve.wait_ge(u_stat, b + 1)
            nc.vector.memset(spare[:, :], 0.0)
            for t in range(TILES):
                last = nc.vector.bn_aggr(mv[:, half, t], stats[:, half, t])
            last.then_inc(u_mv, 1)
            dve.wait_ge(u_mv, b + 1)
            nc.vector.tensor_scalar(var_eps[:, half], mv[:, half, :, 1], 1e-5, None, ALU.add).then_inc(u_var, 1)
            dve.wait_ge(u_rstd, b + 1)
            wait(dve, xn_turned, b - 1)
            wait(dve, un_ready, b - 1)
            for t in range(TILES):
                last = nc.vector.tensor_scalar(xn[:, half, t], u[:, half, t], mv[:, half, t, 0:1],
                                               rstd[:, half, t:t + 1], ALU.subtract, ALU.mult)
            last.then_inc(xn_ready, 1)
            dve.wait_ge(sums_ready, b + 1)
            nc.vector.tensor_scalar(sums_eps[:, half], sums[:, half], 1.0 / D, 1e-6, ALU.mult, ALU.add).then_inc(sums_var, 1)
            dve.wait_ge(driven, b + 1)
            wait(dve, y_done, b - 1)
            nc.vector.tensor_tensor_scan(states[:, half], decay[:, :], drive[:, half], 0.0,
                                         ALU.mult, ALU.add).then_inc(scanned, 1)
            dve.wait_ge(y_done, b + 1)
            wait(dve, acc_out[half], 16 * p)
            nc.vector.tensor_tensor(acc[:, half].rearrange("p t d -> p (t d)"), p_y[half][:, :],
                                    u[:, half].rearrange("p t d -> p (t d)"), ALU.add).then_inc(acc_ready, 1)

        pairs(dve, step)

        dve.wait_ge(late_in, 16 * len(late))
        nc.vector.tensor_copy(w["ident_b"][:, :], w["ident"][:, :])
        nc.vector.tensor_copy(w["q_mask"][:, :, :], q_mask_raw[:, :, :])
        nc.vector.tensor_copy(w["k_mask"][:, :, :], k_mask_raw[:, :, :])
        nc.vector.tensor_copy(w["sel"][:, :, :], sel_raw[:, :, :])
        for l in range(LAYERS):
            for t in range(TILES):
                nc.vector.tensor_tensor(w["cos"][:, l, t], rot_raw[:, 0, t], scales[:, l], ALU.mult)
                for h in range(2):
                    nc.vector.tensor_tensor(w["sin"][:, l, t, :, 32 * h:32 * h + 32], rot_raw[:, 1, t, :, 32 * h:32 * h + 32],
                                            scales[:, l, :, 32 - 32 * h:64 - 32 * h], ALU.mult)
            nc.vector.tensor_scalar(w1_scaled[:, l], w1_raw[:, l], ln_g[:, l:l + 1], None, ALU.mult).then_inc(w1_ready, 1)
        for l in range(LAYERS):
            dve.wait_ge(hi_split, 2 * l + 1)
            nc.vector.tensor_tensor(w["wqkv_lo"][:, l], wqkv_raw[:, l], w["wqkv_hi"][:, l].bitcast(F32), ALU.subtract)
            dve.wait_ge(hi_split, 2 * l + 2)
            nc.vector.tensor_tensor(w["w1_lo"][:, l], w1_scaled[:, l], w["w1_hi"][:, l].bitcast(F32), ALU.subtract)
        dve.wait_ge(folded, 1)
        for l in range(LAYERS):
            for j in range(HB):
                for a in range(2):
                    at = HB * a + j
                    nc.vector.tensor_tensor(w["b1"][0:HROWS[j], l, at:at + 1], p_x[0][0:HROWS[j], 6 * l + at:6 * l + at + 1],
                                            b1_raw[0:HROWS[j], l, at:at + 1], ALU.add)

    @block.scalar
    def _(act):
        act.wait_ge(early_in, 16 * len(early))
        nc.scalar.activation(col[:, 0:1], dt_a[:, 0:1], ACT.Exp, scale=-1.0).then_inc(sigm, 1)
        act.wait_ge(col_done, 5)
        nc.scalar.activation(col[:, 7:8], col[:, 5:6], ACT.Exp).then_inc(expd, 1)

        def step(b, half, p):
            act.wait_ge(xn_ready, b + 1)
            wait(act, sums_var, b - 1)
            for t in range(TILES):
                if t:
                    act.wait_ge(square_done, (TILES - 1) * b + t)
                last = nc.scalar.activation(dump[:, :], xn[:, half, t], ACT.Square, accum_out=sums[:, half, t:t + 1])
                if t < TILES - 1:
                    last.then_inc(square_done, 1)
            last.then_inc(sums_ready, 1)
            act.wait_ge(xn_turned, b + 1)
            nc.scalar.copy(w["xT"][:, bass.ds(b * SEQ, SEQ)], p_x[half][:, :]).then_inc(x_copied, 1)
            act.wait_ge(rms_ready, b + 1)
            wait(act, un_turned, b - 1)
            for t in range(TILES):
                last = nc.scalar.activation(un[:, half, t], xn[:, half, t], ACT.Copy, scale=rms[:, half, t:t + 1])
            last.then_inc(un_ready, 1)
            act.wait_ge(un_turned, b + 1)
            nc.scalar.copy(unT[:, half], p_u[half][:, :]).then_inc(un_copied, 1)
            act.wait_ge(projected, b + 1)
            act.wait_ge(col_done, 4)
            nc.scalar.activation(drive[:, half], p_proj[half][0:S, :], ACT.Copy, scale=col[:, 2:3]).then_inc(driven, 1)
            act.wait_ge(acc_ready, b + 1)
            act.dma_start(acc_tok[b], acc[:, half]).then_inc(acc_out[half], 16)

        pairs(act, step)
        for half in range(2):
            act.wait_ge(acc_out[half], 16 * (NB // 2))
        act.wait_ge(late_in, 16 * len(late))
        for l in range(LAYERS):
            nc.scalar.copy(w["wqkv_hi"][:, l], wqkv_raw[:, l]).then_inc(hi_split, 1)
            act.wait_ge(w1_ready, l + 1)
            nc.scalar.copy(w["w1_hi"][:, l], w1_scaled[:, l]).then_inc(hi_split, 1)

    @block.tensor
    def _(pe):
        pe.wait_ge(early_in, 16 * len(early))
        pe.wait_ge(set_up, 2)
        pe.wait_ge(b_ready, 1)

        def step(b, half, p):
            pe.wait_ge(xn_ready, b + 1)
            wait(pe, x_copied, b - 1)
            for t in range(TILES):
                last = nc.tensor.transpose(p_x[half][:, t * P:(t + 1) * P], xn[:, half, t], w["ident"][:, :])
            last.then_inc(xn_turned, 1)
            pe.wait_ge(un_ready, b + 1)
            for t in range(TILES):
                last = nc.tensor.transpose(p_u[half][:, t * P:(t + 1) * P], un[:, half, t], w["ident"][:, :])
            last.then_inc(un_turned, 1)
            pe.wait_ge(un_copied, b + 1)
            nc.tensor.matmul(p_proj[half][0:S, :], b_mat[:, :], unT[:, half], start=True, stop=True).then_inc(projected, 1)
            pe.wait_ge(scanned, b + 1)
            wait(pe, acc_ready, b - 1)
            for t in range(TILES):
                nc.tensor.matmul(p_y[half][:, t * P:(t + 1) * P], states[:, half, t * P:(t + 1) * P], c_mat[:, :],
                                 start=True, stop=False)
                last = nc.tensor.matmul(p_y[half][:, t * P:(t + 1) * P], ones_row[:, :], d_row[:, :],
                                        start=False, stop=True)
            last.then_inc(y_done, 1)

        pairs(pe, step)
        pe.wait_ge(late_in, 16 * len(late))
        pe.wait_ge(x_copied, NB)
        for l in range(LAYERS):
            for j in range(HB):
                for a in range(2):
                    at = a * HID + HM * j
                    last = nc.tensor.matmul(p_x[0][0:HROWS[j], 6 * l + HB * a + j:6 * l + HB * a + j + 1],
                                            w1_raw[:, l, at:at + HROWS[j]], ln_b[:, l:l + 1], start=True, stop=True)
        last.then_inc(folded, 1)


def layer_steps(nc, ctx, acc_tok, out_tok, w):
    def sb(name, shape, dt=F32):
        return ctx.enter_context(nc.sbuf_tensor(name, shape, dt))

    def pb(name, shape, dt=F32):
        return ctx.enter_context(nc.psum_tensor(name, shape, dt))

    def sem(name):
        return ctx.enter_context(nc.semaphore(name))

    xT = w["xT"]
    h_hi = sb("h_hi", [P, SEQ], F32R)
    h_lo = sb("h_lo", [P, SEQ], F32R)
    sq = sb("sq", [P, 2 * HEADS, DH])
    rot_a = sb("rot_a", [P, 2, HEADS, DH])
    rot_b = sb("rot_b", [P, 2, HEADS, DH])
    qk_n = sb("qk_n", [P, 2 * HEADS, DH])
    ss = sb("ss", [P, 2 * HEADS])
    ss_clip = sb("ss_clip", [P, 2 * HEADS])
    rn = sb("rn", [P, 2 * HEADS])
    qT = sb("qT", [P, PAIRS, P])
    qT_hi = sb("qT_hi", [P, PAIRS, P], F32R)
    kT = sb("kT", [P, PAIRS, WIN + SEQ])
    kT_hi = sb("kT_hi", [P, PAIRS, WIN + SEQ], F32R)
    v_own = sb("v_own", [P, TILES, HEADS, DH + 1])
    v_mix = sb("v_mix", [P, TILES, HEADS, DH + 1])
    mx = sb("mx", [P, 2, PAIRS])
    mx_b = sb("mx_b", [P, 2, 2 * PAIRS], BF16)
    mxT = sb("mxT", [2 * HEADS, P], BF16)
    probs = [sb(f"probs{g}", [P, PAIRS, 2, WIN]) for g in range(2)]
    rden = sb("rden", [P, 2, PAIRS])
    o_tok = sb("o_tok", [P, PAIRS, 2, DH])
    oT = sb("oT", [P, PAIRS, SEQ])
    x1 = sb("x1", [P, SEQ])
    h2 = sb("h2", [P, SEQ + 1])
    stats = sb("stats_f", [P, TILES, 6])
    spare = sb("spare_f", [P, 1])
    mv = sb("mv_f", [P, TILES, 2])
    var_eps = sb("var_eps_f", [P, TILES])
    rs = sb("rs", [P, TILES])
    hn = sb("hn", [P, TILES, P])
    hn_hi = sb("hn_hi", [P, SEQ], F32R)
    hn_lo = sb("hn_lo", [P, SEQ], F32R)
    gate = sb("gate", [HM, HB, SEQ])
    gated = sb("gated", [HM, HB, SEQ])
    x2 = sb("x2", [P, SEQ])
    acc = sb("acc", [P, SEQ])
    result = sb("result", [P, SEQ])

    p_qk = pb("p_qk", [P, 2, INNER])
    p_v = pb("p_v", [P, 512])
    p_t = pb("p_t", [P, 512])
    p_s = pb("p_s", [P, 2, 512])
    p_st = pb("p_st", [P, PAIRS, P])
    p_o = pb("p_o", [P, 512])
    p_oh = p_o[:, 0:PAIRS * (DH + 1)].rearrange("p (j d) -> p j d", j=PAIRS)
    p_mx = p_o[0:2 * HEADS, 384:448].bitcast(BF16)

    zeroed = sem("zeroed")
    h_hi_ready, h_lo_ready = sem("h_hi_ready"), sem("h_lo_ready")
    qk_done, v_done, sq_done, v_copied = sem("qk_done"), sem("v_done"), sem("sq_done"), sem("v_copied")
    rot_done, ss_sum, ss_ready, rn_ready = sem("rot_done"), sem("ss_sum"), sem("ss_ready"), sem("rn_ready")
    added, qkn_ready, turned, full_ready, hi_ready = sem("added"), sem("qkn_ready"), sem("turned"), sem("full_ready"), sem("hi_ready")
    s_done, max_done, mx_hi, mx_ready = sem("s_done"), sem("max_done"), sem("mx_hi"), sem("mx_ready")
    mx_turned, mxT_ready, st_done, p_ready = sem("mx_turned"), sem("mxT_ready"), sem("st_done"), sem("p_ready")
    pv_done, den_ready, o_ready, o_turned, oT_ready = sem("pv_done"), sem("den_ready"), sem("o_ready"), sem("o_turned"), sem("oT_ready")
    wo_done, x1_ready, h2_ready, h2_turned = sem("wo_done"), sem("x1_ready"), sem("h2_ready"), sem("h2_turned")
    stat_done, mv_done, var_ready, rs_ready = sem("stat_done"), sem("mv_done"), sem("var_ready"), sem("rs_ready")
    hn_ready, hn_turned, hn_hi_ready, hn_lo_ready = sem("hn_ready"), sem("hn_turned"), sem("hn_hi_ready"), sem("hn_lo_ready")
    gate_done, up_done, gelu_ready, gated_ready = sem("gate_done"), sem("up_done"), sem("gelu_ready"), sem("gated_ready")
    w2_done, x2_ready, x2_turned, ffn_done = sem("w2_done"), sem("x2_ready"), sem("x2_turned"), sem("ffn_done")
    acc_in, out_stored = sem("acc_in"), sem("out_stored")

    def run(eng, step):
        step(0, 0, None)
        with eng.Fori(1, NB) as s:
            step(s, 0, 0)
        step(NB, 1, 0)
        with eng.Fori(NB + 1, STEPS) as s:
            step(s, 1, 1)
        step(STEPS, None, 1)

    def slots(s, layer, before):
        new, old = layer is not None, before is not None
        for t in range(TILES):
            yield t, 4 * s + t, new, (new if t >= 1 else old), (new if t >= 2 else old)

    block = ctx.enter_context(nc.Block())

    @block.sync
    def _(sp):
        sp.dma_start(acc[:, :].rearrange("p (t d) -> p t d", t=TILES), acc_tok[0]).then_inc(acc_in, 16)
        with sp.Fori(1, NB) as b:
            sp.wait_ge(out_stored, 16 * b)
            sp.dma_start(acc[:, :].rearrange("p (t d) -> p t d", t=TILES), acc_tok[b]).then_inc(acc_in, 16)

    @block.gpsimd
    def _(pool):
        def step(s, layer, before):
            for t, n, new, scored, weighed in slots(s, layer, before):
                if new:
                    pool.wait_ge(rot_done, n + 1)
                    wait(pool, turned, 2 * n)
                    nc.gpsimd.tensor_tensor(qk_n[:, :, :].rearrange("p h d -> p (h d)"),
                                            rot_a[:, :, :, :].rearrange("p a h d -> p (a h d)"),
                                            rot_b[:, :, :, :].rearrange("p a h d -> p (a h d)"), ALU.add).then_inc(added, 1)
                    pool.wait_ge(ss_ready, n + 1)
                    wait(pool, qkn_ready, n)
                    nc.gpsimd.tensor_tensor(rn[:, :], ss_clip[:, :], w["minus_half"][:, :], ALU.pow).then_inc(rn_ready, 1)
                    pool.wait_ge(rn_ready, n + 1)
                    pool.wait_ge(added, n + 1)
                    nc.gpsimd.tensor_tensor(qk_n[:, :, :], qk_n[:, :, :],
                                            rn[:, :].unsqueeze(2).to_broadcast([P, 2 * HEADS, DH]), ALU.mult).then_inc(qkn_ready, 1)
                if before is not None and t == 2:
                    pool.wait_ge(var_ready, s)
                    nc.gpsimd.tensor_tensor(rs[:, :], var_eps[:, :], w["minus_half"][:, 0:TILES], ALU.pow).then_inc(rs_ready, 1)

        run(pool, step)

    @block.scalar
    def _(act):
        def split_rounded(s):
            at = (s % NB) * SEQ
            wait(act, v_done, 4 * s)
            wait(act, ffn_done, s - 1)
            nc.scalar.copy(h_hi[0:WIN, :], xT[0:WIN, bass.ds(at, SEQ)])
            nc.scalar.copy(h_hi[WIN:P, 1:SEQ], xT[WIN:P, bass.ds(at, SEQ - 1)]).then_inc(h_hi_ready, 1)

        def exp(m, g):
            act.wait_ge(st_done, 2 * m + g + 1)
            wait(act, pv_done, 2 * m + g - 1)
            nc.scalar.activation(probs[g][:, :, :, :].rearrange("p j w q -> p (j w q)"),
                                 p_st[:, :, :].rearrange("p j q -> p (j q)"), ACT.Exp, scale=QK_SCALE).then_inc(p_ready, 1)

        def step(s, layer, before):
            for t, n, new, scored, weighed in slots(s, layer, before):
                if new:
                    act.wait_ge(qk_done, n + 1)
                    wait(act, ss_ready, n)
                    nc.scalar.activation(sq[:, :, :].rearrange("p h d -> p (h d)"), p_qk[:, :, :].rearrange("p a d -> p (a d)"),
                                         ACT.Square).then_inc(sq_done, 1)
                if scored:
                    m = n - 1
                    u = (t - 1) % TILES
                    act.wait_ge(full_ready, 2 * m + 1)
                    nc.scalar.copy(qT_hi[:, :, :], qT[:, :, :]).then_inc(hi_ready, 1)
                    act.wait_ge(full_ready, 2 * m + 2)
                    nc.scalar.copy(kT_hi[:, :, WIN + P * u:WIN + P * (u + 1)], kT[:, :, WIN + P * u:WIN + P * (u + 1)]).then_inc(hi_ready, 1)
                if new:
                    act.wait_ge(v_done, n + 1)
                    v_heads = p_v[:, :].rearrange("p (h d) -> p h d", h=HEADS)
                    nc.scalar.copy(v_own[:, t, :, 0:DH], v_heads)
                    last = nc.scalar.copy(v_mix[0:WIN, t, :, 0:DH], v_heads[0:WIN])
                    if t < TILES - 1:
                        last = nc.scalar.copy(v_mix[WIN:P, t + 1, :, 0:DH], v_heads[WIN:P])
                    last.then_inc(v_copied, 1)
                if weighed:
                    m = n - 2
                    u = (t - 2) % TILES
                    act.wait_ge(o_turned, m + 1)
                    nc.scalar.copy(oT[:, :, P * u:P * (u + 1)], p_t[:, :].rearrange("p (j c) -> p j c", j=PAIRS)).then_inc(oT_ready, 1)
                if before is not None and t == 2:
                    act.wait_ge(x1_ready, s)
                    nc.scalar.copy(h2[0:WIN, 0:SEQ], x1[0:WIN, :])
                    nc.scalar.copy(h2[WIN:P, 1:SEQ + 1], x1[WIN:P, :]).then_inc(h2_ready, 1)
                if before is not None and t == 3:
                    act.wait_ge(hn_turned, s)
                    nc.scalar.copy(hn_hi[:, :], p_t[:, :]).then_inc(hn_hi_ready, 1)
                if scored:
                    exp(n - 1, 0)
                    exp(n - 1, 1)
                if before is not None and t == 3:
                    for j in range(HB):
                        r = HROWS[j]
                        act.wait_ge(gate_done, HB * (s - 1) + j + 1)
                        nc.scalar.activation(gate[0:r, j], p_v[0:r, :], ACT.Gelu,
                                             bias=w["b1"][0:r, before, HB + j:HB + j + 1]).then_inc(gelu_ready, 1)
                if new and t == 3 and not (isinstance(s, int) and s + 1 == STEPS):
                    split_rounded(s + 1)
                if before == 1 and t == 3:
                    act.wait_ge(ffn_done, s + 1)
                    act.dma_start(out_tok[s - NB - 1], result[:, :].rearrange("p (t d) -> p t d", t=TILES)).then_inc(out_stored, 16)

        act.wait_ge(zeroed, 8)
        split_rounded(0)
        run(act, step)
        act.wait_ge(out_stored, 16 * NB)

    @block.vector
    def _(dve):
        def split_rest(s):
            at = (s % NB) * SEQ
            dve.wait_ge(h_hi_ready, s + 1)
            nc.vector.tensor_tensor(h_lo[0:WIN, :], xT[0:WIN, bass.ds(at, SEQ)], h_hi[0:WIN, :].bitcast(F32), ALU.subtract)
            nc.vector.tensor_tensor(h_lo[WIN:P, 1:SEQ], xT[WIN:P, bass.ds(at, SEQ - 1)],
                                    h_hi[WIN:P, 1:SEQ].bitcast(F32), ALU.subtract).then_inc(h_lo_ready, 1)

        def weighed_mean(m, g):
            dve.wait_ge(pv_done, 2 * m + g + 1)
            nc.vector.reciprocal(rden[:, g, :], p_oh[:, :, DH]).then_inc(den_ready, 1)
            dve.wait_ge(den_ready, 2 * m + g + 1)
            wait(dve, o_turned, m)
            nc.vector.tensor_tensor(o_tok[:, :, g, :], p_oh[:, :, 0:DH],
                                    rden[:, g, :].unsqueeze(2).to_broadcast([P, PAIRS, DH]), ALU.mult).then_inc(o_ready, 1)

        def maxima(m, g):
            dve.wait_ge(s_done, 2 * m + g + 1)
            nc.vector.tensor_reduce(mx[:, g, :].rearrange("p (a b) -> p a b", a=2),
                                    p_s[:, :, 0:2 * (P + WIN)].rearrange("p a (b c) -> p a b c", b=2), AX.X, ALU.max).then_inc(max_done, 1)

        def sine_part(layer, t, half):
            nc_half = slice(32 * half, 32 * half + 32)
            other = slice(32 - 32 * half, 64 - 32 * half)
            q_k = p_qk[:, :, :].rearrange("p a (h d) -> p a h d", h=HEADS)
            return nc.vector.tensor_tensor(rot_b[:, :, :, nc_half], q_k[:, :, :, other],
                                           w["sin"][:, layer, t, :, nc_half].unsqueeze(2).to_broadcast([P, 2, HEADS, 32]), ALU.mult)

        def step(s, layer, before):
            for t, n, new, scored, weighed in slots(s, layer, before):
                m, u = n - 1, (t - 1) % TILES
                if scored:
                    dve.wait_ge(turned, 2 * m + 1)
                    nc.vector.tensor_copy(qT[:, :, :].rearrange("p j c -> p (j c)"), p_t[:, :]).then_inc(full_ready, 1)
                    dve.wait_ge(turned, 2 * m + 2)
                    nc.vector.tensor_copy(kT[:, :, WIN + P * u:WIN + P * (u + 1)],
                                          p_s[:, 0, :].rearrange("p (j c) -> p j c", j=PAIRS)).then_inc(full_ready, 1)
                if weighed:
                    weighed_mean(n - 2, 0)
                if new:
                    dve.wait_ge(sq_done, n + 1)
                    wait(dve, added, n)
                    nc.vector.tensor_tensor(rot_a[:, :, :, :], p_qk[:, :, :].rearrange("p a (h d) -> p a h d", h=HEADS),
                                            w["cos"][:, layer, t].unsqueeze(2).to_broadcast([P, 2, HEADS, DH]), ALU.mult)
                if scored:
                    maxima(m, 0)
                if weighed:
                    weighed_mean(n - 2, 1)
                if new:
                    sine_part(layer, t, 0)
                if scored:
                    maxima(m, 1)
                    dve.wait_ge(max_done, 2 * m + 2)
                    wait(dve, mx_turned, m)
                    nc.vector.tensor_copy(mx_b[:, 0, :], mx[:, :, :].rearrange("p g j -> p (g j)")).then_inc(mx_hi, 1)
                    dve.wait_ge(mx_hi, m + 1)
                    nc.vector.tensor_tensor(mx_b[:, 1, :], mx[:, :, :].rearrange("p g j -> p (g j)"), mx_b[:, 0, :],
                                            ALU.subtract).then_inc(mx_ready, 1)
                if before is not None and t == 2:
                    x_at = bass.ds((s - 1 - NB * before) * SEQ, SEQ)
                    dve.wait_ge(wo_done, s)
                    nc.vector.tensor_tensor(x1[:, :], p_v[:, :], xT[:, x_at], ALU.add).then_inc(x1_ready, 1)
                if scored:
                    dve.wait_ge(mx_turned, m + 1)
                    nc.vector.tensor_copy(mxT[:, :], p_mx).then_inc(mxT_ready, 1)
                if before is not None and t == 3:
                    dve.wait_ge(hn_hi_ready, s)
                    nc.vector.tensor_tensor(hn_lo[:, :], p_t[:, :], hn_hi[:, :].bitcast(F32), ALU.subtract).then_inc(hn_lo_ready, 1)
                if new:
                    sine_part(layer, t, 1).then_inc(rot_done, 1)
                    dve.wait_ge(sq_done, n + 1)
                    nc.vector.tensor_reduce(ss[:, :], sq[:, :, :], AX.X, ALU.add).then_inc(ss_sum, 1)
                    dve.wait_ge(ss_sum, n + 1)
                    wait(dve, rn_ready, n)
                    nc.vector.tensor_scalar(ss_clip[:, :], ss[:, :], 1e-24, None, ALU.max).then_inc(ss_ready, 1)
                if before is not None and t == 2:
                    dve.wait_ge(h2_turned, s)
                    for c in range(TILES):
                        last = nc.vector.bn_stats(stats[:, c], p_v[:, P * c:P * (c + 1)])
                    last.then_inc(stat_done, 1)
                    dve.wait_ge(stat_done, s)
                    nc.vector.memset(spare[:, :], 0.0)
                    for c in range(TILES):
                        last = nc.vector.bn_aggr(mv[:, c], stats[:, c])
                    last.then_inc(mv_done, 1)
                    dve.wait_ge(mv_done, s)
                    nc.vector.tensor_scalar(var_eps[:, :], mv[:, :, 1], 1e-5, None, ALU.add).then_inc(var_ready, 1)
                    dve.wait_ge(rs_ready, s)
                    for c in range(TILES):
                        last = nc.vector.tensor_scalar(hn[:, c], p_v[:, P * c:P * (c + 1)], mv[:, c, 0:1], rs[:, c:c + 1],
                                                       ALU.subtract, ALU.mult)
                    last.then_inc(hn_ready, 1)
                if before is not None and t == 3:
                    x_at = bass.ds((s - 1 - NB * before) * SEQ, SEQ)
                    for j in range(HB):
                        r = HROWS[j]
                        dve.wait_ge(up_done, HB * (s - 1) + j + 1)
                        dve.wait_ge(gelu_ready, HB * (s - 1) + j + 1)
                        nc.vector.scalar_tensor_tensor(gated[0:r, j], p_t[0:r, :], w["b1"][0:r, before, j:j + 1], gate[0:r, j],
                                                       ALU.add, ALU.mult).then_inc(gated_ready, 1)
                    dve.wait_ge(w2_done, s)
                    if before == 0:
                        nc.vector.scalar_tensor_tensor(xT[:, x_at], p_v[:, :], w["b2"][:, 0:1], x1[:, :],
                                                       ALU.add, ALU.add).then_inc(ffn_done, 1)
                    else:
                        nc.vector.scalar_tensor_tensor(x2[:, :], p_v[:, :], w["b2"][:, 1:2], x1[:, :],
                                                       ALU.add, ALU.add).then_inc(x2_ready, 1)
                        b = s - NB
                        dve.wait_ge(x2_turned, b)
                        dve.wait_ge(acc_in, 16 * b)
                        nc.vector.tensor_tensor(result[:, :], p_t[:, :], acc[:, :], ALU.add).then_inc(ffn_done, 1)
                if new and t == 3 and not (isinstance(s, int) and s + 1 == STEPS):
                    split_rest(s + 1)

        nc.vector.memset(kT[:, :, 0:WIN], 0.0).then_inc(zeroed, 1)
        nc.vector.memset(kT_hi[:, :, 0:WIN].bitcast(F32), 0.0).then_inc(zeroed, 1)
        nc.vector.memset(v_own[:, :, :, DH:DH + 1], 1.0).then_inc(zeroed, 1)
        nc.vector.memset(v_mix[:, :, :, DH:DH + 1], 1.0).then_inc(zeroed, 1)
        nc.vector.memset(v_mix[WIN:P, 0, :, 0:DH], 0.0).then_inc(zeroed, 1)
        nc.vector.memset(h_hi[WIN:P, 0:1].bitcast(F32), 0.0).then_inc(zeroed, 1)
        nc.vector.memset(h_lo[WIN:P, 0:1].bitcast(F32), 0.0).then_inc(zeroed, 1)
        nc.vector.memset(h2[WIN:P, 0:1], 0.0).then_inc(zeroed, 1)
        nc.vector.memset(spare[:, :], 0.0).then_inc(ffn_done, 1)
        split_rest(0)
        run(dve, step)

    @block.tensor
    def _(pe):
        def project(s, layer, t, n, before):
            if t == 0:
                pe.wait_ge(h_hi_ready, s + 1)
                pe.wait_ge(h_lo_ready, s + 1)
            wait(pe, rot_done, n)
            tok = slice(P * t, P * (t + 1))
            for part in range(3):
                dst = [p_qk[:, 0, :], p_qk[:, 1, :], p_v[:, :]][part]
                cols = slice(INNER * part, INNER * (part + 1))
                if part == 2:
                    wait(pe, v_copied, n)
                    if t == 0:
                        wait(pe, ffn_done, s)
                    if t == 3 and before is not None:
                        pe.wait_ge(hn_ready, s)
                nc.tensor.matmul(dst, h_hi[:, tok], w["wqkv_lo"][:, layer, cols], start=True, stop=False)
                nc.tensor.matmul(dst, h_lo[:, tok], w["wqkv_hi"][:, layer, cols], start=False, stop=False)
                last = nc.tensor.matmul(dst, h_hi[:, tok], w["wqkv_hi"][:, layer, cols], start=False, stop=True)
                if part == 1:
                    last.then_inc(qk_done, 1)
            last.then_inc(v_done, 1)

        def turn_qk(m):
            pe.wait_ge(qkn_ready, m + 1)
            wait(pe, oT_ready, m - 1)
            flat = qk_n[:, :, :].rearrange("p h d -> p (h d)")
            for j in range(PAIRS):
                last = nc.tensor.transpose(p_t[:, P * j:P * (j + 1)], flat[:, P * j:P * (j + 1)], w["ident"][:, :])
            last.then_inc(turned, 1)
            wait(pe, max_done, 2 * m)
            for j in range(PAIRS):
                last = nc.tensor.transpose(p_s[:, 0, P * j:P * (j + 1)], flat[:, INNER + P * j:INNER + P * (j + 1)], w["ident"][:, :])
            last.then_inc(turned, 1)

        def scores_by_query(m, u, g):
            rows = slice(DH * g, DH * (g + 1))
            pe.wait_ge(hi_ready, 2 * m + 2)
            wait(pe, max_done, 2 * m + g)
            for bank in range(2):
                nc.tensor.matmul(p_s[:, bank, 0:2 * (P + WIN)].rearrange("p (b c) -> p b c", b=2), w["ident_b"][:, :],
                                 w["q_mask"][:, min(u, 1), :].unsqueeze(1).to_broadcast([P, 2, P + WIN]),
                                 start=True, stop=False, skip_group_check=True)
                for b in range(2):
                    j = 2 * bank + b
                    last = nc.tensor.matmul(p_s[:, bank, b * (P + WIN):(b + 1) * (P + WIN)], qT_hi[rows, j, :],
                                            kT_hi[rows, j, P * u:P * (u + 1) + WIN], start=False, stop=True, skip_group_check=True)
            last.then_inc(s_done, 1)

        def scores_by_key(m, u, g):
            rows = slice(DH * g, DH * (g + 1))
            pe.wait_ge(mxT_ready, m + 1)
            wait(pe, p_ready, 2 * m + g)
            nc.tensor.matmul(p_st[:, :, :], w["ident_b"][:, :], w["k_mask"][:, min(u, 1), :].unsqueeze(1).to_broadcast([P, PAIRS, P]),
                             start=True, stop=False, skip_group_check=True)
            for j in range(PAIRS):
                nc.tensor.matmul(p_st[:, j, :], w["sel"][:, 2 * j + g, :], mxT[:, :], start=False, stop=False, skip_group_check=True)
            even, before, odd = WIN + P * u, P * u, 2 * WIN + P * u
            for j in range(PAIRS):
                nc.tensor.matmul(p_st[0:WIN, j, :], kT[rows, j, even:even + WIN], qT[rows, j, :],
                                 start=False, stop=True, skip_group_check=True)
                nc.tensor.matmul(p_st[WIN:P, j, 0:WIN], kT[rows, j, before:before + WIN], qT[rows, j, 0:WIN],
                                 start=False, stop=True, skip_group_check=True)
                last = nc.tensor.matmul(p_st[WIN:P, j, WIN:P], kT[rows, j, odd:odd + WIN], qT[rows, j, WIN:P],
                                        start=False, stop=True, skip_group_check=True)
            last.then_inc(st_done, 1)

        def weigh(m, u, g):
            pe.wait_ge(p_ready, 2 * m + g + 1)
            wait(pe, o_ready, 2 * m + g)
            for j in range(PAIRS):
                for win, v in ((0, v_mix), (1, v_own)):
                    last = nc.tensor.matmul(p_oh[WIN * win:WIN * (win + 1), j, :], probs[g][:, j, win, :], v[:, u, 2 * j + g, :],
                                            start=True, stop=True, skip_group_check=True)
            last.then_inc(pv_done, 1)

        def step(s, layer, before):
            for t, n, new, scored, weighed in slots(s, layer, before):
                ffn = before is not None
                if new:
                    project(s, layer, t, n, before)
                elif t == 0:
                    pe.wait_ge(ffn_done, s)
                if scored:
                    turn_qk(n - 1)
                if weighed:
                    weigh(n - 2, (t - 2) % TILES, 0)
                if scored:
                    scores_by_query(n - 1, (t - 1) % TILES, 0)
                if weighed:
                    weigh(n - 2, (t - 2) % TILES, 1)
                if scored:
                    scores_by_query(n - 1, (t - 1) % TILES, 1)
                if ffn and t == 2:
                    pe.wait_ge(oT_ready, 4 * s)
                    if new:
                        pe.wait_ge(v_copied, n + 1)
                    for c in range(PAIRS):
                        last = nc.tensor.matmul(p_v[:, :], w["wo"][:, before, c, :], oT[:, c, :], start=(c == 0), stop=(c == PAIRS - 1))
                    last.then_inc(wo_done, 1)
                if weighed:
                    pe.wait_ge(o_ready, 2 * (n - 2) + 2)
                    if scored:
                        pe.wait_ge(full_ready, 2 * (n - 1) + 1)
                    wait(pe, oT_ready, n - 2)
                    for c in range(PAIRS):
                        last = nc.tensor.transpose(p_t[:, P * c:P * (c + 1)], o_tok[:, c, :, :].rearrange("p g d -> p (g d)"), w["ident"][:, :])
                    last.then_inc(o_turned, 1)
                if scored:
                    pe.wait_ge(mx_ready, n)
                    nc.tensor.transpose(p_mx, mx_b[:, :, :].rearrange("p a h -> p (a h)"), w["ident_b"][:, :]).then_inc(mx_turned, 1)
                if ffn and t == 3:
                    pe.wait_ge(hn_ready, s)
                    pe.wait_ge(oT_ready, n - 1 if weighed else 4 * s)
                    for c in range(TILES):
                        last = nc.tensor.transpose(p_t[:, P * c:P * (c + 1)], hn[:, c], w["ident"][:, :])
                    last.then_inc(hn_turned, 1)
                if scored:
                    scores_by_key(n - 1, (t - 1) % TILES, 0)
                if ffn and t == 3:
                    hidden(s, before, 0)
                if ffn and t == 2:
                    pe.wait_ge(h2_ready, s)
                    for c in range(TILES):
                        last = nc.tensor.transpose(p_v[:, P * c:P * (c + 1)], h2[:, P * c:P * (c + 1)], w["ident"][:, :])
                    last.then_inc(h2_turned, 1)
                if scored:
                    scores_by_key(n - 1, (t - 1) % TILES, 1)
                if ffn and t == 3:
                    hidden(s, before, 1)
                    hidden(s, before, 2)
                    pe.wait_ge(gelu_ready, HB * s)
                    pe.wait_ge(gated_ready, HB * s)
                    for j in range(HB):
                        last = nc.tensor.matmul(p_v[:, :], w["w2"][0:HROWS[j], before, j, :], gated[0:HROWS[j], j],
                                                start=(j == 0), stop=(j == HB - 1))
                    last.then_inc(w2_done, 1)
                    if before == 1:
                        pe.wait_ge(x2_ready, s - NB)
                        for c in range(TILES):
                            last = nc.tensor.transpose(p_t[:, P * c:P * (c + 1)], x2[:, P * c:P * (c + 1)], w["ident"][:, :])
                        last.then_inc(x2_turned, 1)

        def hidden(s, layer, j):
            r = HROWS[j]
            if j == 0:
                pe.wait_ge(hn_lo_ready, s)
                pe.wait_ge(v_copied, 4 * s + 4) if layer_new(s) else None
            for a, dst, done, read, name in ((1, p_v, gate_done, gelu_ready, "gate"), (0, p_t, up_done, gated_ready, "up")):
                at = a * HID + HM * j
                if j:
                    pe.wait_ge(read, HB * (s - 1) + j)
                cols = slice(at, at + r)
                nc.tensor.matmul(dst[0:r, :], w["w1_lo"][:, layer, cols], hn_hi[:, :], start=True, stop=False)
                nc.tensor.matmul(dst[0:r, :], w["w1_hi"][:, layer, cols], hn_lo[:, :], start=False, stop=False)
                nc.tensor.matmul(dst[0:r, :], w["w1_hi"][:, layer, cols], hn_hi[:, :], start=False, stop=True).then_inc(done, 1)

        def layer_new(s):
            return not (isinstance(s, int) and s == STEPS)

        run(pe, step)


_INPUTS = {"u": "L0_attn_u", "dt": "L0_attn_dt", "A": "L0_attn_A", "Bmat": "L0_attn_Bmat", "C": "L0_attn_C",
           "D": "L0_attn_D", "norm_w": "L0_attn_norm_w", "wqkv": "L0_ffn_wqkv", "q_scale": "L0_ffn_q_scale",
           "k_scale": "L0_ffn_k_scale", "wo": "L0_ffn_wo", "ln_g": "L0_ffn_ln_g", "ln_b": "L0_ffn_ln_b",
           "w1": "L0_ffn_w1", "b1": "L0_ffn_b1", "w2": "L0_ffn_w2", "b2": "L0_ffn_b2"}


def kernel(**inputs):
    import concourse.bacc as bacc
    from concourse.bass_utils import run_bass_kernel_spmd

    nc = bacc.Bacc("TRN2", target_bir_lowering=False, num_devices=1)
    rot_cos, rot_sin = rotary_tables()
    q_mask, k_mask = masks()
    arrays = {name: np.ascontiguousarray(inputs[full]) for name, full in _INPUTS.items()}
    arrays |= {"rot_cos": rot_cos, "rot_sin": rot_sin, "q_mask": q_mask, "k_mask": k_mask,
               "sel": selectors(), "ident": np.eye(P, dtype=np.float32)}
    aps = {name: nc.dram_tensor(f"in_{name}", a.shape, F32, kind="ExternalInput").ap() for name, a in arrays.items()}
    out = nc.dram_tensor("out", (NB, SEQ, D), F32, kind="ExternalOutput").ap()
    acc = nc.dram_tensor("first_sums", (NB, SEQ, D), F32, kind="Internal").ap()
    build(nc, aps, out, acc)
    r = run_bass_kernel_spmd(nc, [{f"in_{name}": a for name, a in arrays.items()}], core_ids=[0])
    return r.results[0]["out"]
```

```python
from contextlib import ExitStack

import numpy as np

import concourse.bass as bass
from concourse import mybir

F32 = mybir.dt.float32
F32R = mybir.dt.float32r
BF16 = mybir.dt.bfloat16
ALU = mybir.AluOpType
ACT = mybir.ActivationFunctionType
AX = mybir.AxisListType

P = 128
NB = 16
SEQ = 512
D = 128
TILES = SEQ // P
HEADS = 8
PAIRS = HEADS // 2
DH = 64
WIN = 64
INNER = HEADS * DH
HID = D * 4 * 2 // 3
LAYERS = 2
S = 64
HB = 3
HM = -(-HID // HB)
HROWS = [min(HM, HID - HM * j) for j in range(HB)]
QK_SCALE = 8.0
MASKED = -1e30
STEPS = LAYERS * NB


def rotary_tables():
    half = np.arange(0, DH, 2, dtype=np.float32)
    inv_freq = (np.float32(1.0) / np.float32(10000.0) ** (half / np.float32(DH))).astype(np.float32)
    t = np.arange(SEQ, dtype=np.float32)
    freqs = t[:, None] * inv_freq[None, :]
    base = (half + np.float32(0.4 * DH)) / np.float32(1.4 * DH)
    power = (t - SEQ // 2) / np.float32(WIN // 2)
    scale = (base[None, :] ** power[:, None]).astype(np.float32)
    cos, sin = np.cos(freqs), np.sin(freqs)
    both = lambda a, b: np.concatenate([a, b], axis=-1)
    c = np.stack([both(cos * scale, cos * scale), both(cos / scale, cos / scale)], 1)
    s = np.stack([both(-sin * scale, sin * scale), both(-sin / scale, sin / scale)], 1)
    lay = lambda a: np.ascontiguousarray(
        a.astype(np.float32).reshape(TILES, P, 2, DH).transpose(1, 0, 2, 3))
    return lay(c), lay(s)


def masks():
    r, c = np.arange(P)[:, None], np.arange(P + WIN)[None, :]
    seen = (r <= c) & (c <= r + WIN)
    q_mask = np.stack([seen & (c >= WIN), seen], 1)
    k, q = np.arange(WIN)[:, None], np.arange(WIN)[None, :]
    own, before, none = k <= q, k >= q, np.zeros((WIN, WIN), bool)
    first = np.concatenate([np.concatenate([own, before], 1), np.concatenate([none, own], 1)], 0)
    later = np.concatenate([np.concatenate([own, before], 1), np.concatenate([before, own], 1)], 0)
    k_mask = np.stack([first, later], 1)
    add = lambda m: np.where(m, np.float32(0), np.float32(MASKED)).astype(np.float32)
    return add(q_mask), add(k_mask)


def selectors():
    sel = np.zeros((2 * HEADS, HEADS, P), np.float32)
    for h in range(HEADS):
        row = 4 * (h % 2) + h // 2
        sel[row, h] = sel[HEADS + row, h] = -1.0
    return sel


def wait(eng, sem, value):
    if not (isinstance(value, int) and value <= 0):
        eng.wait_ge(sem, value)


def build(nc, i, out, acc_dram):
    u_tok = i["u"].rearrange("b (t p) d -> b p t d", p=P)
    out_tok = out.rearrange("b (t p) d -> b p t d", p=P)
    acc_tok = acc_dram.rearrange("b (t p) d -> b p t d", p=P)

    with ExitStack() as ctx:
        def sb(name, shape, dt=F32):
            return ctx.enter_context(nc.sbuf_tensor(name, shape, dt))

        w = {
            "ident": sb("ident", [P, P]),
            "ident_b": sb("ident_b", [P, P], BF16),
            "q_mask": sb("q_mask", [P, 2, P + WIN], BF16),
            "k_mask": sb("k_mask", [P, 2, P], BF16),
            "sel": sb("sel", [2 * HEADS, HEADS, P], BF16),
            "minus_half": sb("minus_half", [P, 16]),
            "cos": sb("cos", [P, LAYERS, TILES, 2, DH]),
            "sin": sb("sin", [P, LAYERS, TILES, 2, DH]),
            "wqkv_hi": sb("wqkv_hi", [P, LAYERS, 3 * INNER], F32R),
            "wqkv_lo": sb("wqkv_lo", [P, LAYERS, 3 * INNER], F32R),
            "w1_hi": sb("w1_hi", [P, LAYERS, 2 * HID], F32R),
            "w1_lo": sb("w1_lo", [P, LAYERS, 2 * HID], F32R),
            "wo": sb("wo", [P, LAYERS, PAIRS, D]),
            "w2": sb("w2", [HM, LAYERS, HB, D]),
            "b1": sb("b1", [HM, LAYERS, 2 * HB]),
            "b2": sb("b2", [P, LAYERS]),
            "xT": sb("xT", [P, NB * SEQ]),
        }
        with ExitStack() as first:
            first_pass(nc, first, i, u_tok, acc_tok, w)
        with ExitStack() as layers:
            layer_steps(nc, layers, acc_tok, out_tok, w)


def first_pass(nc, ctx, i, u_tok, acc_tok, w):
    def sb(name, shape, dt=F32):
        return ctx.enter_context(nc.sbuf_tensor(name, shape, dt))

    def pb(name, shape, dt=F32):
        return ctx.enter_context(nc.psum_tensor(name, shape, dt))

    def sem(name):
        return ctx.enter_context(nc.semaphore(name))

    wqkv_raw = sb("wqkv_raw", [P, LAYERS, 3 * INNER])
    w1_raw = sb("w1_raw", [P, LAYERS, 2 * HID])
    w1_scaled = sb("w1_scaled", [P, LAYERS, 2 * HID])
    q_mask_raw = sb("q_mask_raw", [P, 2, P + WIN])
    k_mask_raw = sb("k_mask_raw", [P, 2, P])
    sel_raw = sb("sel_raw", [2 * HEADS, HEADS, P])
    rot_raw = sb("rot_raw", [P, 2, TILES, 2, DH])
    scales = sb("scales", [P, LAYERS, 2, DH])
    b1_raw = sb("b1_raw", [HM, LAYERS, 2 * HB])
    ln_g = sb("ln_g", [P, LAYERS])
    ln_b = sb("ln_b", [P, LAYERS])
    b_raw = sb("b_raw", [P, S])
    b_mat = sb("b_mat", [P, S])
    norm_w = sb("norm_w", [P, 1])
    c_mat = sb("c_mat", [S, D])
    d_row = sb("d_row", [1, D])
    ones_row = sb("ones_row", [1, P])
    dt_a = sb("dt_a", [S, 2])
    col = sb("col", [S, 24])
    decay = sb("decay", [S, SEQ])

    u = sb("u", [P, 2, TILES, D])
    stats = sb("stats", [P, 2, TILES, 6])
    mv = sb("mv", [P, 2, TILES, 2])
    var_eps = sb("var_eps", [P, 2, TILES])
    rstd = sb("rstd", [P, 2, TILES])
    xn = sb("xn", [P, 2, TILES, D])
    dump = sb("dump", [P, D])
    spare = sb("spare", [P, 1])
    sums = sb("sums", [P, 2, TILES])
    sums_eps = sb("sums_eps", [P, 2, TILES])
    rms = sb("rms", [P, 2, TILES])
    un = sb("un", [P, 2, TILES, D])
    unT = sb("unT", [P, 2, SEQ])
    drive = sb("drive", [S, 2, SEQ])
    states = sb("states", [S, 2, SEQ])
    acc = sb("acc_first", [P, 2, TILES, D])

    p_x = [pb(f"p_x{h}", [P, SEQ]) for h in range(2)]
    p_u = [pb(f"p_u{h}", [P, SEQ]) for h in range(2)]
    p_proj = [pb(f"p_proj{h}", [P, SEQ]) for h in range(2)]
    p_y = [pb(f"p_y{h}", [P, SEQ]) for h in range(2)]

    early_in, late_in, weight_in, u_in = sem("early_in"), sem("late_in"), sem("weight_in"), [sem(f"u_in{h}") for h in range(2)]
    set_up, col_done, sigm, expd, b_ready = sem("set_up"), sem("col_done"), sem("sigm"), sem("expd"), sem("b_ready")
    hi_split, lo_split, w1_ready, folded = sem("hi_split"), sem("lo_split"), sem("w1_ready"), sem("folded")
    u_stat, u_mv, u_var, u_rstd = sem("u_stat"), sem("u_mv"), sem("u_var"), sem("u_rstd")
    xn_ready, sums_ready, sums_var, rms_ready = sem("xn_ready"), sem("sums_ready"), sem("sums_var"), sem("rms_ready")
    un_ready, xn_turned, un_turned = sem("un_ready"), sem("xn_turned"), sem("un_turned")
    x_copied, un_copied, projected, driven = sem("x_copied"), sem("un_copied"), sem("projected"), sem("driven")
    scanned, y_done, acc_ready, acc_out = sem("scanned"), sem("y_done"), sem("acc_ready"), [sem(f"acc_out{h}") for h in range(2)]
    square_done = sem("square_done")

    early = []
    late = []
    vec = lambda a: a.rearrange("(a b) -> a b", b=1)
    early += [(w["ident"][:, :], i["ident"]), (dt_a[:, 0:1], vec(i["dt"])), (dt_a[:, 1:2], vec(i["A"])),
              (b_raw[:, :], i["Bmat"]), (norm_w[:, :], vec(i["norm_w"])), (c_mat[:, :], i["C"]),
              (d_row[:, :], i["D"].rearrange("(a b) -> a b", a=1))]
    late += [(rot_raw[:, 0], i["rot_cos"]), (rot_raw[:, 1], i["rot_sin"]),
             (q_mask_raw[:, :, :], i["q_mask"]), (k_mask_raw[:, :, :], i["k_mask"]), (sel_raw[:, :, :], i["sel"])]
    for l in range(LAYERS):
        late += [(scales[:, l, 0, :], i["q_scale"][l:l + 1, :].partition_broadcast(P)),
                 (scales[:, l, 1, :], i["k_scale"][l:l + 1, :].partition_broadcast(P)),
                 (ln_g[:, l:l + 1], vec(i["ln_g"][l])), (ln_b[:, l:l + 1], vec(i["ln_b"][l])),
                 (w["b2"][:, l:l + 1], vec(i["b2"][l])),
                 (w["wo"][:, l], i["wo"][l].rearrange("(c p) d -> p c d", p=P)),
                 (wqkv_raw[:, l], i["wqkv"][l]), (w1_raw[:, l], i["w1"][l])]
        for j in range(HB):
            late.append((w["w2"][0:HROWS[j], l, j], i["w2"][l, HM * j:HM * j + HROWS[j], :]))
            for a in range(2):
                at = a * HID + HM * j
                late.append((b1_raw[0:HROWS[j], l, HB * a + j:HB * a + j + 1], vec(i["b1"][l, at:at + HROWS[j]])))

    def pairs(eng, step):
        for half in range(2):
            step(half, half, 0)
        with eng.Fori(1, NB // 2) as p:
            for half in range(2):
                step(2 * p + half, half, p)

    block = ctx.enter_context(nc.Block())

    @block.sync
    def _(sp):
        sp.dma_start(u[:, 0], u_tok[0]).then_inc(u_in[0], 16)
        for dst, src in early:
            sp.dma_start(dst, src).then_inc(early_in, 16)
        sp.dma_start(u[:, 1], u_tok[1]).then_inc(u_in[1], 16)
        for dst, src in late:
            sp.dma_start(dst, src).then_inc(late_in, 16)
        with sp.Fori(1, NB // 2) as p:
            for half in range(2):
                sp.wait_ge(acc_ready, 2 * p + (half - 1))
                sp.dma_start(u[:, half], u_tok[2 * p + half]).then_inc(u_in[half], 16)

    @block.gpsimd
    def _(pool):
        pool.memset(w["minus_half"][:, :], -0.5).then_inc(set_up, 1)
        pool.memset(ones_row[:, :], 1.0).then_inc(set_up, 1)
        pool.wait_ge(set_up, 2)

        def step(b, half, p):
            pool.wait_ge(u_var, b + 1)
            nc.gpsimd.tensor_tensor(rstd[:, half], var_eps[:, half], w["minus_half"][:, 0:TILES],
                                    ALU.pow).then_inc(u_rstd, 1)
            pool.wait_ge(sums_var, b + 1)
            nc.gpsimd.tensor_tensor(rms[:, half], sums_eps[:, half], w["minus_half"][:, 0:TILES],
                                    ALU.pow).then_inc(rms_ready, 1)

        pairs(pool, step)

    @block.vector
    def _(dve):
        count = [0]

        def chained(instruction):
            instruction.then_inc(col_done, 1)
            count[0] += 1
            dve.wait_ge(col_done, count[0])

        dve.wait_ge(early_in, 16 * len(early))
        nc.vector.tensor_scalar(b_mat[:, :], b_raw[:, :], norm_w[:, 0:1], None, ALU.mult).then_inc(b_ready, 1)
        dve.wait_ge(sigm, 1)
        chained(nc.vector.tensor_scalar(col[:, 1:2], col[:, 0:1], 1.0, None, ALU.add))
        chained(nc.vector.reciprocal(col[:, 2:3], col[:, 1:2]))
        chained(nc.vector.tensor_scalar(col[:, 3:4], dt_a[:, 1:2], -1.0, None, ALU.mult))
        chained(nc.vector.tensor_tensor(col[:, 4:5], col[:, 3:4], dt_a[:, 1:2], ALU.min))
        chained(nc.vector.tensor_tensor(col[:, 5:6], col[:, 4:5], col[:, 2:3], ALU.mult))
        chained(nc.vector.tensor_scalar(col[:, 6:7], col[:, 5:6], -0.35, None, ALU.max))
        chained(nc.vector.memset(col[:, 8:9], 1.0 / 9))
        for order in range(8, -1, -1):
            at = 8 + (9 - order)
            chained(nc.vector.tensor_scalar(col[:, at:at + 1], col[:, at - 1:at], col[:, 6:7], 1.0, ALU.mult, ALU.add))
            if order > 1:
                chained(nc.vector.tensor_scalar(col[:, 8 + (9 - order):9 + (9 - order)],
                                                col[:, 8 + (9 - order):9 + (9 - order)], 1.0 / order, None, ALU.mult))
        chained(nc.vector.tensor_scalar(col[:, 18:19], col[:, 5:6], -0.35, None, ALU.is_gt))
        dve.wait_ge(expd, 1)
        chained(nc.vector.tensor_tensor(col[:, 19:20], col[:, 17:18], col[:, 7:8], ALU.subtract))
        chained(nc.vector.tensor_tensor(col[:, 20:21], col[:, 19:20], col[:, 18:19], ALU.mult))
        chained(nc.vector.tensor_tensor(col[:, 21:22], col[:, 20:21], col[:, 7:8], ALU.add))
        chained(nc.vector.memset(decay[:, :], 1.0))
        chained(nc.vector.tensor_scalar(decay[:, :], decay[:, :], col[:, 21:22], None, ALU.mult))

        def step(b, half, p):
            dve.wait_ge(u_in[half], 16 * p + 16)
            for t in range(TILES):
                last = nc.vector.bn_stats(stats[:, half, t], u[:, half, t])
            last.then_inc(u_stat, 1)
            dve.wait_ge(u_stat, b + 1)
            nc.vector.memset(spare[:, :], 0.0)
            for t in range(TILES):
                last = nc.vector.bn_aggr(mv[:, half, t], stats[:, half, t])
            last.then_inc(u_mv, 1)
            dve.wait_ge(u_mv, b + 1)
            nc.vector.tensor_scalar(var_eps[:, half], mv[:, half, :, 1], 1e-5, None, ALU.add).then_inc(u_var, 1)
            dve.wait_ge(u_rstd, b + 1)
            wait(dve, xn_turned, b - 1)
            wait(dve, un_ready, b - 1)
            for t in range(TILES):
                last = nc.vector.tensor_scalar(xn[:, half, t], u[:, half, t], mv[:, half, t, 0:1],
                                               rstd[:, half, t:t + 1], ALU.subtract, ALU.mult)
            last.then_inc(xn_ready, 1)
            dve.wait_ge(sums_ready, b + 1)
            nc.vector.tensor_scalar(sums_eps[:, half], sums[:, half], 1.0 / D, 1e-6, ALU.mult, ALU.add).then_inc(sums_var, 1)
            dve.wait_ge(driven, b + 1)
            wait(dve, y_done, b - 1)
            nc.vector.tensor_tensor_scan(states[:, half], decay[:, :], drive[:, half], 0.0,
                                         ALU.mult, ALU.add).then_inc(scanned, 1)
            dve.wait_ge(y_done, b + 1)
            wait(dve, acc_out[half], 16 * p)
            nc.vector.tensor_tensor(acc[:, half].rearrange("p t d -> p (t d)"), p_y[half][:, :],
                                    u[:, half].rearrange("p t d -> p (t d)"), ALU.add).then_inc(acc_ready, 1)

        pairs(dve, step)

        dve.wait_ge(late_in, 16 * len(late))
        nc.vector.tensor_copy(w["ident_b"][:, :], w["ident"][:, :])
        nc.vector.tensor_copy(w["q_mask"][:, :, :], q_mask_raw[:, :, :])
        nc.vector.tensor_copy(w["k_mask"][:, :, :], k_mask_raw[:, :, :])
        nc.vector.tensor_copy(w["sel"][:, :, :], sel_raw[:, :, :])
        for l in range(LAYERS):
            for t in range(TILES):
                nc.vector.tensor_tensor(w["cos"][:, l, t], rot_raw[:, 0, t], scales[:, l], ALU.mult)
                for h in range(2):
                    nc.vector.tensor_tensor(w["sin"][:, l, t, :, 32 * h:32 * h + 32], rot_raw[:, 1, t, :, 32 * h:32 * h + 32],
                                            scales[:, l, :, 32 - 32 * h:64 - 32 * h], ALU.mult)
            nc.vector.tensor_scalar(w1_scaled[:, l], w1_raw[:, l], ln_g[:, l:l + 1], None, ALU.mult).then_inc(w1_ready, 1)
        for l in range(LAYERS):
            dve.wait_ge(hi_split, 2 * l + 1)
            nc.vector.tensor_tensor(w["wqkv_lo"][:, l], wqkv_raw[:, l], w["wqkv_hi"][:, l].bitcast(F32), ALU.subtract)
            dve.wait_ge(hi_split, 2 * l + 2)
            nc.vector.tensor_tensor(w["w1_lo"][:, l], w1_scaled[:, l], w["w1_hi"][:, l].bitcast(F32), ALU.subtract)
        dve.wait_ge(folded, 1)
        for l in range(LAYERS):
            for j in range(HB):
                for a in range(2):
                    at = HB * a + j
                    nc.vector.tensor_tensor(w["b1"][0:HROWS[j], l, at:at + 1], p_x[0][0:HROWS[j], 6 * l + at:6 * l + at + 1],
                                            b1_raw[0:HROWS[j], l, at:at + 1], ALU.add)

    @block.scalar
    def _(act):
        act.wait_ge(early_in, 16 * len(early))
        nc.scalar.activation(col[:, 0:1], dt_a[:, 0:1], ACT.Exp, scale=-1.0).then_inc(sigm, 1)
        act.wait_ge(col_done, 5)
        nc.scalar.activation(col[:, 7:8], col[:, 5:6], ACT.Exp).then_inc(expd, 1)

        def step(b, half, p):
            act.wait_ge(xn_ready, b + 1)
            wait(act, sums_var, b - 1)
            for t in range(TILES):
                if t:
                    act.wait_ge(square_done, (TILES - 1) * b + t)
                last = nc.scalar.activation(dump[:, :], xn[:, half, t], ACT.Square, accum_out=sums[:, half, t:t + 1])
                if t < TILES - 1:
                    last.then_inc(square_done, 1)
            last.then_inc(sums_ready, 1)
            act.wait_ge(xn_turned, b + 1)
            nc.scalar.copy(w["xT"][:, bass.ds(b * SEQ, SEQ)], p_x[half][:, :]).then_inc(x_copied, 1)
            act.wait_ge(rms_ready, b + 1)
            wait(act, un_turned, b - 1)
            for t in range(TILES):
                last = nc.scalar.activation(un[:, half, t], xn[:, half, t], ACT.Copy, scale=rms[:, half, t:t + 1])
            last.then_inc(un_ready, 1)
            act.wait_ge(un_turned, b + 1)
            nc.scalar.copy(unT[:, half], p_u[half][:, :]).then_inc(un_copied, 1)
            act.wait_ge(projected, b + 1)
            act.wait_ge(col_done, 4)
            nc.scalar.activation(drive[:, half], p_proj[half][0:S, :], ACT.Copy, scale=col[:, 2:3]).then_inc(driven, 1)
            act.wait_ge(acc_ready, b + 1)
            act.dma_start(acc_tok[b], acc[:, half]).then_inc(acc_out[half], 16)

        pairs(act, step)
        for half in range(2):
            act.wait_ge(acc_out[half], 16 * (NB // 2))
        act.wait_ge(late_in, 16 * len(late))
        for l in range(LAYERS):
            nc.scalar.copy(w["wqkv_hi"][:, l], wqkv_raw[:, l]).then_inc(hi_split, 1)
            act.wait_ge(w1_ready, l + 1)
            nc.scalar.copy(w["w1_hi"][:, l], w1_scaled[:, l]).then_inc(hi_split, 1)

    @block.tensor
    def _(pe):
        pe.wait_ge(early_in, 16 * len(early))
        pe.wait_ge(set_up, 2)
        pe.wait_ge(b_ready, 1)

        def step(b, half, p):
            pe.wait_ge(xn_ready, b + 1)
            wait(pe, x_copied, b - 1)
            for t in range(TILES):
                last = nc.tensor.transpose(p_x[half][:, t * P:(t + 1) * P], xn[:, half, t], w["ident"][:, :])
            last.then_inc(xn_turned, 1)
            pe.wait_ge(un_ready, b + 1)
            for t in range(TILES):
                last = nc.tensor.transpose(p_u[half][:, t * P:(t + 1) * P], un[:, half, t], w["ident"][:, :])
            last.then_inc(un_turned, 1)
            pe.wait_ge(un_copied, b + 1)
            nc.tensor.matmul(p_proj[half][0:S, :], b_mat[:, :], unT[:, half], start=True, stop=True).then_inc(projected, 1)
            pe.wait_ge(scanned, b + 1)
            wait(pe, acc_ready, b - 1)
            for t in range(TILES):
                nc.tensor.matmul(p_y[half][:, t * P:(t + 1) * P], states[:, half, t * P:(t + 1) * P], c_mat[:, :],
                                 start=True, stop=False)
                last = nc.tensor.matmul(p_y[half][:, t * P:(t + 1) * P], ones_row[:, :], d_row[:, :],
                                        start=False, stop=True)
            last.then_inc(y_done, 1)

        pairs(pe, step)
        pe.wait_ge(late_in, 16 * len(late))
        pe.wait_ge(x_copied, NB)
        for l in range(LAYERS):
            for j in range(HB):
                for a in range(2):
                    at = a * HID + HM * j
                    last = nc.tensor.matmul(p_x[0][0:HROWS[j], 6 * l + HB * a + j:6 * l + HB * a + j + 1],
                                            w1_raw[:, l, at:at + HROWS[j]], ln_b[:, l:l + 1], start=True, stop=True)
        last.then_inc(folded, 1)


def layer_steps(nc, ctx, acc_tok, out_tok, w):
    def sb(name, shape, dt=F32):
        return ctx.enter_context(nc.sbuf_tensor(name, shape, dt))

    def pb(name, shape, dt=F32):
        return ctx.enter_context(nc.psum_tensor(name, shape, dt))

    def sem(name):
        return ctx.enter_context(nc.semaphore(name))

    xT = w["xT"]
    h_hi = sb("h_hi", [P, SEQ], F32R)
    h_lo = sb("h_lo", [P, SEQ], F32R)
    sq = sb("sq", [P, 2 * HEADS, DH])
    rot_a = sb("rot_a", [P, 2, HEADS, DH])
    rot_b = sb("rot_b", [P, 2, HEADS, DH])
    qk_n = sb("qk_n", [P, 2, 2 * HEADS, DH])
    ss = sb("ss", [P, 2 * HEADS])
    ss_clip = sb("ss_clip", [P, 2 * HEADS])
    rn = sb("rn", [P, 2 * HEADS])
    qT = sb("qT", [P, PAIRS, P])
    qT_hi = sb("qT_hi", [P, PAIRS, P], F32R)
    kT = sb("kT", [P, PAIRS, WIN + SEQ])
    kT_hi = sb("kT_hi", [P, PAIRS, WIN + SEQ], F32R)
    v_own = sb("v_own", [P, TILES, HEADS, DH + 1])
    v_mix = sb("v_mix", [P, TILES, HEADS, DH + 1])
    mx = sb("mx", [P, 2, PAIRS])
    mx_b = sb("mx_b", [P, 2, 2 * PAIRS], BF16)
    mxT = sb("mxT", [2 * HEADS, P], BF16)
    probs = [sb(f"probs{g}", [P, PAIRS, 2, WIN]) for g in range(2)]
    rden = sb("rden", [P, 2, PAIRS])
    o_tok = sb("o_tok", [P, PAIRS, 2, DH])
    oT = sb("oT", [P, PAIRS, SEQ])
    x1 = sb("x1", [P, SEQ])
    h2 = sb("h2", [P, SEQ + 1])
    stats = sb("stats_f", [P, TILES, 6])
    spare = sb("spare_f", [P, 1])
    mv = sb("mv_f", [P, TILES, 2])
    var_eps = sb("var_eps_f", [P, TILES])
    rs = sb("rs", [P, TILES])
    h2_tok = sb("h2_tok", [P, TILES, P])
    hn = sb("hn", [P, TILES, P])
    hn_hi = sb("hn_hi", [P, SEQ], F32R)
    hn_lo = sb("hn_lo", [P, SEQ], F32R)
    gate = sb("gate", [HM, HB, SEQ])
    gated = sb("gated", [HM, HB, SEQ])
    x2 = sb("x2", [P, SEQ])
    acc = sb("acc", [P, SEQ])
    result = sb("result", [P, SEQ])

    p_qk = pb("p_qk", [P, 2, INNER])
    p_v = pb("p_v", [P, 512])
    p_t = pb("p_t", [P, 512])
    p_bank = {bank: pb(f"p_bank{bank}", [P, 512])[:, :] for bank in (4, 5, 6)}
    p_query = [p_bank[bank][:, 0:2 * (P + WIN)] for bank in (4, 5, 6, 4)]
    p_st = [p_bank[bank].rearrange("p (j q) -> p j q", j=PAIRS) for bank in (6, 5)]
    p_o = pb("p_o", [P, 512])
    p_oh = p_o[:, 0:PAIRS * (DH + 1)].rearrange("p (j d) -> p j d", j=PAIRS)
    p_mx = p_o[0:2 * HEADS, 384:448].bitcast(BF16)

    zeroed = sem("zeroed")
    h_hi_ready, h_lo_ready = sem("h_hi_ready"), sem("h_lo_ready")
    qk_done, v_done, sq_done, v_copied = sem("qk_done"), sem("v_done"), sem("sq_done"), sem("v_copied")
    rot_done, ss_sum, ss_ready, rn_ready = sem("rot_done"), sem("ss_sum"), sem("ss_ready"), sem("rn_ready")
    added, qkn_ready, q_turned, k_turned = sem("added"), sem("qkn_ready"), sem("q_turned"), sem("k_turned")
    qT_ready, q_hi_ready, kT_ready = sem("qT_ready"), sem("q_hi_ready"), sem("kT_ready")
    v_mixed = [sem(f"v_mixed{t}") for t in range(TILES)]
    s_done, max_done, mx_hi, mx_ready = sem("s_done"), sem("max_done"), sem("mx_hi"), sem("mx_ready")
    mx_turned, mxT_ready, st_done, p_ready = sem("mx_turned"), sem("mxT_ready"), sem("st_done"), sem("p_ready")
    pv_done, den_ready, o_ready, o_turned, oT_ready = sem("pv_done"), sem("den_ready"), sem("o_ready"), sem("o_turned"), sem("oT_ready")
    wo_done, x1_ready, h2_ready, h2_turned, h2_copied = sem("wo_done"), sem("x1_ready"), sem("h2_ready"), sem("h2_turned"), sem("h2_copied")
    stat_done, mv_done, var_ready, rs_ready = sem("stat_done"), sem("mv_done"), sem("var_ready"), sem("rs_ready")
    hn_ready, hn_turned, hn_hi_ready, hn_lo_ready = sem("hn_ready"), sem("hn_turned"), sem("hn_hi_ready"), sem("hn_lo_ready")
    gate_done, up_done, gelu_ready, gated_ready = sem("gate_done"), sem("up_done"), sem("gelu_ready"), sem("gated_ready")
    w2_done, x2_ready, x2_turned, ffn_done = sem("w2_done"), sem("x2_ready"), sem("x2_turned"), sem("ffn_done")
    acc_in, result_ready, out_stored = sem("acc_in"), sem("result_ready"), sem("out_stored")

    def run(eng, step):
        step(0, 0, None, None)
        step(1, 0, 0, None)
        with eng.Fori(2, NB) as s:
            step(s, 0, 0, 0)
        step(NB, 1, 0, 0)
        step(NB + 1, 1, 1, 0)
        with eng.Fori(NB + 2, STEPS) as s:
            step(s, 1, 1, 1)
        step(STEPS, None, 1, 1)
        step(STEPS + 1, None, None, 1)

    def slots(s, layer, before, tail):
        new, old = layer is not None, before is not None
        for t in range(TILES):
            yield (t, 4 * s + t, new, (new if t >= 2 else old), (new if t >= 3 else old),
                   old and t == 3, tail is not None and t < 3)

    block = ctx.enter_context(nc.Block())

    @block.sync
    def _(sp):
        def step(s, layer, before, tail):
            for t, n, new, scored, weighed, begun, ended in slots(s, layer, before, tail):
                if new:
                    sp.wait_ge(v_copied, n + 1)
                    sp.dma_start(v_mix[0:WIN, t, :, 0:DH], v_own[0:WIN, t, :, 0:DH]).then_inc(v_mixed[t], 16)
                    if t < TILES - 1:
                        wait(sp, pv_done, 2 * (n - 3) + 2)
                        sp.dma_start(v_mix[WIN:P, t + 1, :, 0:DH], v_own[WIN:P, t, :, 0:DH]).then_inc(v_mixed[t], 16)
                if tail == 1 and t == 2 and not (isinstance(s, int) and s == STEPS + 1):
                    b = s - NB - 1
                    sp.wait_ge(out_stored, 16 * b)
                    sp.dma_start(acc[:, :].rearrange("p (t d) -> p t d", t=TILES), acc_tok[b]).then_inc(acc_in, 16)

        sp.dma_start(acc[:, :].rearrange("p (t d) -> p t d", t=TILES), acc_tok[0]).then_inc(acc_in, 16)
        run(sp, step)

    @block.gpsimd
    def _(pool):
        def step(s, layer, before, tail):
            for t, n, new, scored, weighed, begun, ended in slots(s, layer, before, tail):
                if new:
                    pool.wait_ge(ss_ready, n + 1)
                    wait(pool, qkn_ready, n)
                    nc.gpsimd.tensor_tensor(rn[:, :], ss_clip[:, :], w["minus_half"][:, :], ALU.pow).then_inc(rn_ready, 1)
                    pool.wait_ge(rot_done, n + 1)
                    wait(pool, k_turned, n - 1)
                    nc.gpsimd.tensor_tensor(qk_n[:, t % 2].rearrange("p h d -> p (h d)"),
                                            rot_a[:, :, :, :].rearrange("p a h d -> p (a h d)"),
                                            rot_b[:, :, :, :].rearrange("p a h d -> p (a h d)"), ALU.add).then_inc(added, 1)
                    pool.wait_ge(rn_ready, n + 1)
                    pool.wait_ge(added, n + 1)
                    nc.gpsimd.tensor_tensor(qk_n[:, t % 2], qk_n[:, t % 2],
                                            rn[:, :].unsqueeze(2).to_broadcast([P, 2 * HEADS, DH]), ALU.mult).then_inc(qkn_ready, 1)
                if begun:
                    pool.wait_ge(var_ready, s)
                    nc.gpsimd.tensor_tensor(rs[:, :], var_eps[:, :], w["minus_half"][:, 0:TILES], ALU.pow).then_inc(rs_ready, 1)

        run(pool, step)

    @block.scalar
    def _(act):
        def split_rounded(s):
            at = (s % NB) * SEQ
            wait(act, qk_done, 4 * s)
            nc.scalar.copy(h_hi[0:WIN, :], xT[0:WIN, bass.ds(at, SEQ)])
            nc.scalar.copy(h_hi[WIN:P, 1:SEQ], xT[WIN:P, bass.ds(at, SEQ - 1)]).then_inc(h_hi_ready, 1)

        def copy_o(r, v):
            act.wait_ge(o_turned, r + 1)
            nc.scalar.copy(oT[:, :, P * v:P * (v + 1)], p_t[:, :].rearrange("p (j c) -> p j c", j=PAIRS)).then_inc(oT_ready, 1)

        def gelu(k, layer, j):
            r = HROWS[j]
            act.wait_ge(gate_done, HB * (k - 1) + j + 1)
            nc.scalar.activation(gate[0:r, j], p_v[0:r, :], ACT.Gelu,
                                 bias=w["b1"][0:r, layer, HB + j:HB + j + 1]).then_inc(gelu_ready, 1)

        def exp(m, g):
            act.wait_ge(st_done, 2 * m + g + 1)
            wait(act, pv_done, 2 * m + g - 1)
            nc.scalar.activation(probs[g][:, :, :, :].rearrange("p j w q -> p (j w q)"),
                                 p_st[g].rearrange("p j q -> p (j q)"), ACT.Exp, scale=QK_SCALE).then_inc(p_ready, 1)

        def step(s, layer, before, tail):
            for t, n, new, scored, weighed, begun, ended in slots(s, layer, before, tail):
                m, u = n - 2, (t - 2) % TILES
                if scored:
                    act.wait_ge(k_turned, m + 1)
                    tile = slice(WIN + P * u, WIN + P * (u + 1))
                    k_blocks = p_bank[4].rearrange("p (j c) -> p j c", j=PAIRS)
                    nc.scalar.copy(kT_hi[:, :, tile], k_blocks)
                    nc.scalar.copy(kT[:, :, tile], k_blocks).then_inc(kT_ready, 1)
                if new:
                    act.wait_ge(v_done, n + 1)
                    nc.scalar.copy(v_own[:, t, :, 0:DH], p_v[:, :].rearrange("p (h d) -> p h d", h=HEADS)).then_inc(v_copied, 1)
                if ended and t == 1:
                    gelu(s - 1, tail, 0)
                if ended and t == 2:
                    gelu(s - 1, tail, 2)
                if weighed and not begun and ended and t >= 1:
                    copy_o(n - 3, (t - 3) % TILES)
                if new:
                    act.wait_ge(qk_done, n + 1)
                    wait(act, ss_ready, n)
                    nc.scalar.activation(sq[:, :, :].rearrange("p h d -> p (h d)"), p_qk[:, :, :].rearrange("p a d -> p (a d)"),
                                         ACT.Square).then_inc(sq_done, 1)
                if new and t == 3 and not (isinstance(s, int) and s + 1 == STEPS):
                    split_rounded(s + 1)
                if weighed and not begun and not (ended and t >= 1):
                    copy_o(n - 3, (t - 3) % TILES)
                if begun:
                    act.wait_ge(x1_ready, s)
                    nc.scalar.copy(h2[0:WIN, 0:SEQ], x1[0:WIN, :])
                    nc.scalar.copy(h2[WIN:P, 1:SEQ + 1], x1[WIN:P, :]).then_inc(h2_ready, 1)
                    if weighed:
                        copy_o(n - 3, 0)
                elif ended and t == 1:
                    gelu(s - 1, tail, 1)
                if scored:
                    exp(m, 0)
                if begun:
                    act.wait_ge(h2_turned, s)
                    nc.scalar.copy(h2_tok[:, :, :].rearrange("p t d -> p (t d)"), p_v[:, :]).then_inc(h2_copied, 1)
                if ended and t == 0:
                    act.wait_ge(hn_turned, s - 1)
                    nc.scalar.copy(hn_hi[:, :], p_v[:, :]).then_inc(hn_hi_ready, 1)
                if scored:
                    exp(m, 1)
                if tail == 1 and t == 2:
                    b = s - NB - 2
                    act.wait_ge(result_ready, b + 1)
                    act.dma_start(out_tok[b], result[:, :].rearrange("p (t d) -> p t d", t=TILES)).then_inc(out_stored, 16)

        act.wait_ge(zeroed, 8)
        split_rounded(0)
        run(act, step)
        act.wait_ge(out_stored, 16 * NB)

    @block.vector
    def _(dve):
        def split_rest(s):
            at = (s % NB) * SEQ
            dve.wait_ge(h_hi_ready, s + 1)
            nc.vector.tensor_tensor(h_lo[0:WIN, :], xT[0:WIN, bass.ds(at, SEQ)], h_hi[0:WIN, :].bitcast(F32), ALU.subtract)
            nc.vector.tensor_tensor(h_lo[WIN:P, 1:SEQ], xT[WIN:P, bass.ds(at, SEQ - 1)],
                                    h_hi[WIN:P, 1:SEQ].bitcast(F32), ALU.subtract).then_inc(h_lo_ready, 1)

        def weighed_mean(m, g):
            dve.wait_ge(pv_done, 2 * m + g + 1)
            nc.vector.reciprocal(rden[:, g, :], p_oh[:, :, DH]).then_inc(den_ready, 1)
            dve.wait_ge(den_ready, 2 * m + g + 1)
            wait(dve, o_turned, m)
            nc.vector.tensor_tensor(o_tok[:, :, g, :], p_oh[:, :, 0:DH],
                                    rden[:, g, :].unsqueeze(2).to_broadcast([P, PAIRS, DH]), ALU.mult).then_inc(o_ready, 1)

        def maxima(m, unit):
            g, b = unit // 2, unit % 2
            dve.wait_ge(s_done, 4 * m + unit + 1)
            nc.vector.tensor_reduce(mx[:, g, 2 * b:2 * b + 2],
                                    p_query[unit].rearrange("p (b c) -> p b c", b=2), AX.X, ALU.max).then_inc(max_done, 1)

        def sine_part(layer, t, half):
            nc_half = slice(32 * half, 32 * half + 32)
            other = slice(32 - 32 * half, 64 - 32 * half)
            q_k = p_qk[:, :, :].rearrange("p a (h d) -> p a h d", h=HEADS)
            return nc.vector.tensor_tensor(rot_b[:, :, :, nc_half], q_k[:, :, :, other],
                                           w["sin"][:, layer, t, :, nc_half].unsqueeze(2).to_broadcast([P, 2, HEADS, 32]), ALU.mult)

        def cosine_part(layer, t):
            return nc.vector.tensor_tensor(rot_a[:, :, :, :], p_qk[:, :, :].rearrange("p a (h d) -> p a h d", h=HEADS),
                                           w["cos"][:, layer, t].unsqueeze(2).to_broadcast([P, 2, HEADS, DH]), ALU.mult)

        def gated_values(k, layer, j):
            r = HROWS[j]
            dve.wait_ge(up_done, HB * (k - 1) + j + 1)
            dve.wait_ge(gelu_ready, HB * (k - 1) + j + 1)
            nc.vector.scalar_tensor_tensor(gated[0:r, j], p_t[0:r, :], w["b1"][0:r, layer, j:j + 1], gate[0:r, j],
                                           ALU.add, ALU.mult).then_inc(gated_ready, 1)

        def step(s, layer, before, tail):
            for t, n, new, scored, weighed, begun, ended in slots(s, layer, before, tail):
                m = n - 2
                if scored:
                    dve.wait_ge(q_turned, m + 1)
                    nc.vector.tensor_copy(qT[:, :, :].rearrange("p j c -> p (j c)"), p_t[:, :]).then_inc(qT_ready, 1)
                    dve.wait_ge(qT_ready, m + 1)
                    nc.vector.tensor_copy(qT_hi[:, :, :], qT[:, :, :]).then_inc(q_hi_ready, 1)
                if weighed:
                    weighed_mean(n - 3, 0)
                if scored:
                    for unit in range(3):
                        maxima(m, unit)
                if weighed:
                    weighed_mean(n - 3, 1)
                if scored:
                    maxima(m, 3)
                    dve.wait_ge(max_done, 4 * m + 4)
                    wait(dve, mx_turned, m)
                    nc.vector.tensor_copy(mx_b[:, 0, :], mx[:, :, :].rearrange("p g j -> p (g j)")).then_inc(mx_hi, 1)
                    dve.wait_ge(mx_hi, m + 1)
                    nc.vector.tensor_tensor(mx_b[:, 1, :], mx[:, :, :].rearrange("p g j -> p (g j)"), mx_b[:, 0, :],
                                            ALU.subtract).then_inc(mx_ready, 1)
                    dve.wait_ge(mx_turned, m + 1)
                    nc.vector.tensor_copy(mxT[:, :], p_mx).then_inc(mxT_ready, 1)
                if ended and t == 0:
                    dve.wait_ge(rs_ready, s - 1)
                    wait(dve, hn_turned, s - 2)
                    for c in range(TILES):
                        last = nc.vector.tensor_scalar(hn[:, c], h2_tok[:, c], mv[:, c, 0:1], rs[:, c:c + 1],
                                                       ALU.subtract, ALU.mult)
                    last.then_inc(hn_ready, 1)
                if ended and t == 1:
                    gated_values(s - 1, tail, 0)
                if ended and t == 2:
                    gated_values(s - 1, tail, 2)
                if new:
                    dve.wait_ge(sq_done, n + 1)
                    nc.vector.tensor_reduce(ss[:, :], sq[:, :, :], AX.X, ALU.add).then_inc(ss_sum, 1)
                if new:
                    wait(dve, added, n)
                    sine_part(layer, t, 0)
                    dve.wait_ge(ss_sum, n + 1)
                    wait(dve, rn_ready, n)
                    nc.vector.tensor_scalar(ss_clip[:, :], ss[:, :], 1e-24, None, ALU.max).then_inc(ss_ready, 1)
                    sine_part(layer, t, 1)
                if begun:
                    x_at = bass.ds((s - 1 - NB * before) * SEQ, SEQ)
                    dve.wait_ge(wo_done, s)
                    nc.vector.tensor_tensor(x1[:, :], p_v[:, :], xT[:, x_at], ALU.add).then_inc(x1_ready, 1)
                if ended and t == 0:
                    dve.wait_ge(hn_hi_ready, s - 1)
                    nc.vector.tensor_tensor(hn_lo[:, :], p_v[:, :], hn_hi[:, :].bitcast(F32), ALU.subtract).then_inc(hn_lo_ready, 1)
                if ended and t == 1:
                    gated_values(s - 1, tail, 1)
                if new:
                    cosine_part(layer, t).then_inc(rot_done, 1)
                if new and t == 3 and not (isinstance(s, int) and s + 1 == STEPS):
                    split_rest(s + 1)
                if begun:
                    dve.wait_ge(h2_copied, s)
                    for c in range(TILES):
                        last = nc.vector.bn_stats(stats[:, c], h2_tok[:, c])
                    last.then_inc(stat_done, 1)
                    dve.wait_ge(stat_done, s)
                    nc.vector.memset(spare[:, :], 0.0)
                    for c in range(TILES):
                        last = nc.vector.bn_aggr(mv[:, c], stats[:, c])
                    last.then_inc(mv_done, 1)
                    dve.wait_ge(mv_done, s)
                    nc.vector.tensor_scalar(var_eps[:, :], mv[:, :, 1], 1e-5, None, ALU.add).then_inc(var_ready, 1)
                if ended and t == 2:
                    dve.wait_ge(w2_done, s - 1)
                    if tail == 0:
                        nc.vector.scalar_tensor_tensor(xT[:, bass.ds((s - 2) * SEQ, SEQ)], p_v[:, :], w["b2"][:, 0:1], x1[:, :],
                                                       ALU.add, ALU.add).then_inc(ffn_done, 1)
                    else:
                        b = s - NB - 2
                        nc.vector.scalar_tensor_tensor(x2[:, :], p_v[:, :], w["b2"][:, 1:2], x1[:, :],
                                                       ALU.add, ALU.add).then_inc(x2_ready, 1)
                        dve.wait_ge(x2_turned, b + 1)
                        dve.wait_ge(acc_in, 16 * (b + 1))
                        nc.vector.tensor_tensor(result[:, :], p_v[:, :], acc[:, :], ALU.add).then_inc(result_ready, 1)

        nc.vector.memset(kT[:, :, 0:WIN], 0.0).then_inc(zeroed, 1)
        nc.vector.memset(kT_hi[:, :, 0:WIN].bitcast(F32), 0.0).then_inc(zeroed, 1)
        nc.vector.memset(v_own[:, :, :, DH:DH + 1], 1.0).then_inc(zeroed, 1)
        nc.vector.memset(v_mix[:, :, :, DH:DH + 1], 1.0).then_inc(zeroed, 1)
        nc.vector.memset(v_mix[WIN:P, 0, :, 0:DH], 0.0).then_inc(zeroed, 1)
        nc.vector.memset(h_hi[WIN:P, 0:1].bitcast(F32), 0.0).then_inc(zeroed, 1)
        nc.vector.memset(h_lo[WIN:P, 0:1].bitcast(F32), 0.0).then_inc(zeroed, 1)
        nc.vector.memset(h2[WIN:P, 0:1], 0.0).then_inc(zeroed, 1)
        split_rest(0)
        run(dve, step)

    @block.tensor
    def _(pe):
        def project(s, layer, t, n, parts):
            tok = slice(P * t, P * (t + 1))
            for part in parts:
                dst = [p_qk[:, 0, :], p_qk[:, 1, :], p_v[:, :]][part]
                cols = slice(INNER * part, INNER * (part + 1))
                nc.tensor.matmul(dst, h_hi[:, tok], w["wqkv_lo"][:, layer, cols], start=True, stop=False)
                nc.tensor.matmul(dst, h_lo[:, tok], w["wqkv_hi"][:, layer, cols], start=False, stop=False)
                last = nc.tensor.matmul(dst, h_hi[:, tok], w["wqkv_hi"][:, layer, cols], start=False, stop=True)
            return last

        def project_q(s, layer, t, n):
            wait(pe, rot_done, n)
            project(s, layer, t, n, (0,))

        def project_k(s, layer, t, n):
            project(s, layer, t, n, (1,)).then_inc(qk_done, 1)

        def project_v(s, layer, t, n, tail):
            if t == 0:
                pe.wait_ge(h_hi_ready, s + 1)
                pe.wait_ge(h_lo_ready, s + 1)
            wait(pe, v_copied, n)
            if tail is not None:
                k = s - 1
                if t == 0:
                    pe.wait_ge(h2_copied, k)
                if t == 1:
                    pe.wait_ge(hn_lo_ready, k)
                if t == 2:
                    pe.wait_ge(gelu_ready, HB * (k - 1) + 2)
                if t == 3:
                    wait_tail_read(s, tail)
            project(s, layer, t, n, (2,)).then_inc(v_done, 1)

        def wait_tail_read(s, tail):
            if tail == 0:
                pe.wait_ge(ffn_done, s - 1)
            else:
                pe.wait_ge(result_ready, s - NB - 1)

        def turn_qk(s, m, t, tail):
            pe.wait_ge(qkn_ready, m + 1)
            wait(pe, oT_ready, m - 1)
            if tail is not None and t == 2:
                pe.wait_ge(gated_ready, HB * (s - 2) + 2)
            if tail is not None and t == 3:
                pe.wait_ge(gated_ready, HB * (s - 1))
            flat = qk_n[:, t % 2].rearrange("p h d -> p (h d)")
            for j in range(PAIRS):
                last = nc.tensor.transpose(p_t[:, P * j:P * (j + 1)], flat[:, P * j:P * (j + 1)], w["ident"][:, :])
            last.then_inc(q_turned, 1)
            wait(pe, max_done, 4 * m)
            for j in range(PAIRS):
                last = nc.tensor.transpose(p_bank[4][:, P * j:P * (j + 1)], flat[:, INNER + P * j:INNER + P * (j + 1)], w["ident"][:, :])
            last.then_inc(k_turned, 1)

        def scores_by_query(m, u, units):
            for unit in units:
                g, b = unit // 2, unit % 2
                rows = slice(DH * g, DH * (g + 1))
                if unit == 0:
                    pe.wait_ge(q_hi_ready, m + 1)
                    pe.wait_ge(kT_ready, m + 1)
                if unit == 1:
                    wait(pe, p_ready, 2 * m)
                if unit == 3:
                    pe.wait_ge(max_done, 4 * m + 1)
                nc.tensor.matmul(p_query[unit].rearrange("p (b c) -> p b c", b=2), w["ident_b"][:, :],
                                 w["q_mask"][:, min(u, 1), :].unsqueeze(1).to_broadcast([P, 2, P + WIN]),
                                 start=True, stop=False, skip_group_check=True)
                for c in range(2):
                    last = nc.tensor.matmul(p_query[unit][:, c * (P + WIN):(c + 1) * (P + WIN)], qT_hi[rows, 2 * b + c, :],
                                            kT_hi[rows, 2 * b + c, P * u:P * (u + 1) + WIN], start=False, stop=True, skip_group_check=True)
                last.then_inc(s_done, 1)

        def scores_by_key(m, u, g):
            rows = slice(DH * g, DH * (g + 1))
            if g == 0:
                pe.wait_ge(mxT_ready, m + 1)
            dst = p_st[g]
            nc.tensor.matmul(dst, w["ident_b"][:, :], w["k_mask"][:, min(u, 1), :].unsqueeze(1).to_broadcast([P, PAIRS, P]),
                             start=True, stop=False, skip_group_check=True)
            for j in range(PAIRS):
                nc.tensor.matmul(dst[:, j, :], w["sel"][:, 2 * j + g, :], mxT[:, :], start=False, stop=False, skip_group_check=True)
            even, before, odd = WIN + P * u, P * u, 2 * WIN + P * u
            for j in range(PAIRS):
                nc.tensor.matmul(dst[0:WIN, j, :], kT[rows, j, even:even + WIN], qT[rows, j, :],
                                 start=False, stop=True, skip_group_check=True)
                nc.tensor.matmul(dst[WIN:P, j, 0:WIN], kT[rows, j, before:before + WIN], qT[rows, j, 0:WIN],
                                 start=False, stop=True, skip_group_check=True)
                last = nc.tensor.matmul(dst[WIN:P, j, WIN:P], kT[rows, j, odd:odd + WIN], qT[rows, j, WIN:P],
                                        start=False, stop=True, skip_group_check=True)
            last.then_inc(st_done, 1)

        def weigh(s, m, u, g):
            if g == 0:
                pe.wait_ge(v_mixed[u], (32 if u < TILES - 1 else 16) * (s + 1 if u == 0 else s))
            pe.wait_ge(p_ready, 2 * m + g + 1)
            wait(pe, o_ready, 2 * m + g)
            for j in range(PAIRS):
                for win, v in ((0, v_mix), (1, v_own)):
                    last = nc.tensor.matmul(p_oh[WIN * win:WIN * (win + 1), j, :], probs[g][:, j, win, :], v[:, u, 2 * j + g, :],
                                            start=True, stop=True, skip_group_check=True)
            last.then_inc(pv_done, 1)

        def hidden(k, layer, j, a):
            r = HROWS[j]
            dst, done = (p_v, gate_done) if a else (p_t, up_done)
            at = a * HID + HM * j
            cols = slice(at, at + r)
            nc.tensor.matmul(dst[0:r, :], w["w1_lo"][:, layer, cols], hn_hi[:, :], start=True, stop=False)
            nc.tensor.matmul(dst[0:r, :], w["w1_hi"][:, layer, cols], hn_lo[:, :], start=False, stop=False)
            nc.tensor.matmul(dst[0:r, :], w["w1_hi"][:, layer, cols], hn_hi[:, :], start=False, stop=True).then_inc(done, 1)

        def turn(dst, src, done):
            for c in range(TILES):
                last = nc.tensor.transpose(dst[:, P * c:P * (c + 1)], src(c), w["ident"][:, :])
            last.then_inc(done, 1)

        def step(s, layer, before, tail):
            for t, n, new, scored, weighed, begun, ended in slots(s, layer, before, tail):
                u, v, k = (t - 2) % TILES, (t - 3) % TILES, s - 1
                if scored:
                    turn_qk(s, n - 2, t, tail)
                if weighed:
                    weigh(s, n - 3, v, 0)
                if new:
                    project_v(s, layer, t, n, tail)
                if scored:
                    scores_by_query(n - 2, u, (0, 1, 2))
                if weighed:
                    weigh(s, n - 3, v, 1)
                if scored:
                    scores_by_query(n - 2, u, (3,))
                if ended and t >= 1:
                    if new:
                        pe.wait_ge(v_copied, n + 1)
                    pe.wait_ge(*((hn_lo_ready, k) if t == 1 else (gelu_ready, HB * (k - 1) + 2)))
                    hidden(k, tail, 0 if t == 1 else 2, 1)
                if weighed and ended and t >= 1:
                    turn_o(n, scored)
                if new:
                    project_q(s, layer, t, n)
                if new and not (ended and t >= 1):
                    project_k(s, layer, t, n)
                if scored:
                    turn_maxima(n, weighed)
                if new and ended and t >= 1:
                    project_k(s, layer, t, n)
                if weighed and not begun and not (ended and t >= 1):
                    turn_o(n, scored)
                if ended and t >= 1:
                    if weighed:
                        pe.wait_ge(oT_ready, n - 2)
                    elif t == 2:
                        pe.wait_ge(gated_ready, HB * (k - 1) + 2)
                    hidden(k, tail, 0 if t == 1 else 2, 0)
                if begun:
                    pe.wait_ge(oT_ready, 4 * s)
                    if new:
                        pe.wait_ge(v_copied, n + 1)
                    elif tail is not None:
                        wait_tail_read(s, tail)
                    for c in range(PAIRS):
                        last = nc.tensor.matmul(p_v[:, :], w["wo"][:, before, c, :], oT[:, c, :], start=(c == 0), stop=(c == PAIRS - 1))
                    last.then_inc(wo_done, 1)
                    if weighed:
                        turn_o(n, scored)
                if scored:
                    scores_by_key(n - 2, u, 0)
                if begun:
                    pe.wait_ge(h2_ready, s)
                    turn(p_v, lambda c: h2[:, P * c:P * (c + 1)], h2_turned)
                if ended and t == 0:
                    pe.wait_ge(hn_ready, k)
                    pe.wait_ge(*((v_copied, n + 1) if new else (h2_copied, k)))
                    turn(p_v, lambda c: hn[:, c], hn_turned)
                if ended and t == 1:
                    pe.wait_ge(gelu_ready, HB * (k - 1) + 1)
                    hidden(k, tail, 1, 1)
                    pe.wait_ge(gated_ready, HB * (k - 1) + 1)
                    hidden(k, tail, 1, 0)
                if ended and t == 2:
                    pe.wait_ge(gated_ready, HB * k)
                    for j in range(HB):
                        last = nc.tensor.matmul(p_v[:, :], w["w2"][0:HROWS[j], tail, j, :], gated[0:HROWS[j], j],
                                                start=(j == 0), stop=(j == HB - 1))
                    last.then_inc(w2_done, 1)
                if scored:
                    scores_by_key(n - 2, u, 1)
                if ended and t == 2 and tail == 1:
                    pe.wait_ge(x2_ready, s - NB - 1)
                    turn(p_v, lambda c: x2[:, P * c:P * (c + 1)], x2_turned)

        def turn_maxima(n, weighed):
            if weighed:
                pe.wait_ge(o_ready, 2 * (n - 3) + 2)
            pe.wait_ge(mx_ready, n - 1)
            nc.tensor.transpose(p_mx, mx_b[:, :, :].rearrange("p a h -> p (a h)"), w["ident_b"][:, :]).then_inc(mx_turned, 1)

        def turn_o(n, scored):
            pe.wait_ge(o_ready, 2 * (n - 3) + 2)
            if scored:
                pe.wait_ge(qT_ready, n - 1)
            wait(pe, oT_ready, n - 3)
            turn(p_t, lambda c: o_tok[:, c, :, :].rearrange("p g d -> p (g d)"), o_turned)

        run(pe, step)


_INPUTS = {"u": "L0_attn_u", "dt": "L0_attn_dt", "A": "L0_attn_A", "Bmat": "L0_attn_Bmat", "C": "L0_attn_C",
           "D": "L0_attn_D", "norm_w": "L0_attn_norm_w", "wqkv": "L0_ffn_wqkv", "q_scale": "L0_ffn_q_scale",
           "k_scale": "L0_ffn_k_scale", "wo": "L0_ffn_wo", "ln_g": "L0_ffn_ln_g", "ln_b": "L0_ffn_ln_b",
           "w1": "L0_ffn_w1", "b1": "L0_ffn_b1", "w2": "L0_ffn_w2", "b2": "L0_ffn_b2"}


def kernel(**inputs):
    import concourse.bacc as bacc
    from concourse.bass_utils import run_bass_kernel_spmd

    nc = bacc.Bacc("TRN2", target_bir_lowering=False, num_devices=1)
    rot_cos, rot_sin = rotary_tables()
    q_mask, k_mask = masks()
    arrays = {name: np.ascontiguousarray(inputs[full]) for name, full in _INPUTS.items()}
    arrays |= {"rot_cos": rot_cos, "rot_sin": rot_sin, "q_mask": q_mask, "k_mask": k_mask,
               "sel": selectors(), "ident": np.eye(P, dtype=np.float32)}
    aps = {name: nc.dram_tensor(f"in_{name}", a.shape, F32, kind="ExternalInput").ap() for name, a in arrays.items()}
    out = nc.dram_tensor("out", (NB, SEQ, D), F32, kind="ExternalOutput").ap()
    acc = nc.dram_tensor("first_sums", (NB, SEQ, D), F32, kind="Internal").ap()
    build(nc, aps, out, acc)
    r = run_bass_kernel_spmd(nc, [{f"in_{name}": a for name, a in arrays.items()}], core_ids=[0])
    return r.results[0]["out"]
```

```python
from contextlib import ExitStack

import numpy as np

import concourse.bass as bass
from concourse import mybir

F32 = mybir.dt.float32
F32R = mybir.dt.float32r
BF16 = mybir.dt.bfloat16
ALU = mybir.AluOpType
ACT = mybir.ActivationFunctionType
AX = mybir.AxisListType

P = 128
NB = 16
SEQ = 512
D = 128
TILES = SEQ // P
HEADS = 8
PAIRS = HEADS // 2
DH = 64
WIN = 64
INNER = HEADS * DH
HID = D * 4 * 2 // 3
LAYERS = 2
S = 64
HB = 3
HM = -(-HID // HB)
HROWS = [min(HM, HID - HM * j) for j in range(HB)]
QK_SCALE = 8.0
MASKED = -1e30
STEPS = LAYERS * NB


def rotary_tables():
    half = np.arange(0, DH, 2, dtype=np.float32)
    inv_freq = (np.float32(1.0) / np.float32(10000.0) ** (half / np.float32(DH))).astype(np.float32)
    t = np.arange(SEQ, dtype=np.float32)
    freqs = t[:, None] * inv_freq[None, :]
    base = (half + np.float32(0.4 * DH)) / np.float32(1.4 * DH)
    power = (t - SEQ // 2) / np.float32(WIN // 2)
    scale = (base[None, :] ** power[:, None]).astype(np.float32)
    cos, sin = np.cos(freqs), np.sin(freqs)
    both = lambda a, b: np.concatenate([a, b], axis=-1)
    c = np.stack([both(cos * scale, cos * scale), both(cos / scale, cos / scale)], 1)
    s = np.stack([both(-sin * scale, sin * scale), both(-sin / scale, sin / scale)], 1)
    lay = lambda a: np.ascontiguousarray(
        a.astype(np.float32).reshape(TILES, P, 2, DH).transpose(1, 0, 2, 3))
    return lay(c), lay(s)


def masks():
    r, c = np.arange(P)[:, None], np.arange(P + WIN)[None, :]
    seen = (r <= c) & (c <= r + WIN)
    q_mask = np.stack([seen & (c >= WIN), seen], 1)
    k, q = np.arange(WIN)[:, None], np.arange(WIN)[None, :]
    own, before, none = k <= q, k >= q, np.zeros((WIN, WIN), bool)
    first = np.concatenate([np.concatenate([own, before], 1), np.concatenate([none, own], 1)], 0)
    later = np.concatenate([np.concatenate([own, before], 1), np.concatenate([before, own], 1)], 0)
    k_mask = np.stack([first, later], 1)
    add = lambda m: np.where(m, np.float32(0), np.float32(MASKED)).astype(np.float32)
    return add(q_mask), add(k_mask)


def selectors():
    sel = np.zeros((2 * HEADS, HEADS, P), np.float32)
    for h in range(HEADS):
        row = 4 * (h % 2) + h // 2
        sel[row, h] = sel[HEADS + row, h] = -1.0
    return sel


def wait(eng, sem, value):
    if not (isinstance(value, int) and value <= 0):
        eng.wait_ge(sem, value)


def build(nc, i, out, acc_dram):
    u_tok = i["u"].rearrange("b (t p) d -> b p t d", p=P)
    out_tok = out.rearrange("b (t p) d -> b p t d", p=P)
    acc_tok = acc_dram.rearrange("b (t p) d -> b p t d", p=P)

    with ExitStack() as ctx:
        def sb(name, shape, dt=F32):
            return ctx.enter_context(nc.sbuf_tensor(name, shape, dt))

        w = {
            "ident": sb("ident", [P, P]),
            "ident_b": sb("ident_b", [P, P], BF16),
            "q_mask": sb("q_mask", [P, 2, P + WIN], BF16),
            "k_mask": sb("k_mask", [P, 2, P], BF16),
            "sel": sb("sel", [2 * HEADS, HEADS, P], BF16),
            "minus_half": sb("minus_half", [P, 16]),
            "cos": sb("cos", [P, LAYERS, TILES, 2, DH]),
            "sin": sb("sin", [P, LAYERS, TILES, 2, DH]),
            "wqkv_hi": sb("wqkv_hi", [P, LAYERS, 3 * INNER], F32R),
            "wqkv_lo": sb("wqkv_lo", [P, LAYERS, 3 * INNER], F32R),
            "w1_hi": sb("w1_hi", [P, LAYERS, 2 * HID], F32R),
            "w1_lo": sb("w1_lo", [P, LAYERS, 2 * HID], F32R),
            "wo_hi": sb("wo_hi", [P, LAYERS, PAIRS, D], F32R),
            "wo_lo": sb("wo_lo", [P, LAYERS, PAIRS, D], F32R),
            "w2_hi": sb("w2_hi", [HM, LAYERS, HB, D], F32R),
            "w2_lo": sb("w2_lo", [HM, LAYERS, HB, D], F32R),
            "b1": sb("b1", [HM, LAYERS, 2 * HB]),
            "b2": sb("b2", [P, LAYERS]),
            "xT": sb("xT", [P, NB * SEQ]),
        }
        with ExitStack() as first:
            first_pass(nc, first, i, u_tok, acc_tok, w)
        with ExitStack() as layers:
            layer_steps(nc, layers, acc_tok, out_tok, w)


LAG = 5


def first_pass(nc, ctx, i, u_tok, acc_tok, w):
    def sb(name, shape, dt=F32):
        return ctx.enter_context(nc.sbuf_tensor(name, shape, dt))

    def pb(name, shape, dt=F32):
        return ctx.enter_context(nc.psum_tensor(name, shape, dt))

    def sem(name):
        return ctx.enter_context(nc.semaphore(name))

    wqkv_raw = sb("wqkv_raw", [P, LAYERS, 3 * INNER])
    w1_raw = sb("w1_raw", [P, LAYERS, 2 * HID])
    wo_raw = sb("wo_raw", [P, LAYERS, PAIRS, D])
    w2_raw = sb("w2_raw", [HM, LAYERS, HB, D])
    w1_scaled = sb("w1_scaled", [P, LAYERS, 2 * HID])
    q_mask_raw = sb("q_mask_raw", [P, 2, P + WIN])
    k_mask_raw = sb("k_mask_raw", [P, 2, P])
    sel_raw = sb("sel_raw", [2 * HEADS, HEADS, P])
    rot_raw = sb("rot_raw", [P, 2, TILES, 2, DH])
    scales = sb("scales", [P, LAYERS, 2, DH])
    b1_raw = sb("b1_raw", [HM, LAYERS, 2 * HB])
    ln_g = sb("ln_g", [P, LAYERS])
    ln_b = sb("ln_b", [P, LAYERS])
    b_raw = sb("b_raw", [P, S])
    b_mat = sb("b_mat", [P, S])
    norm_w = sb("norm_w", [P, 1])
    c_d = sb("c_d", [S + 1, D])
    dt_a = sb("dt_a", [S, 2])
    col = sb("col", [S, 24])
    decay = sb("decay", [S, SEQ])

    u = sb("u", [P, NB * SEQ])
    stats = sb("stats", [P, 2, TILES, 6])
    mv = sb("mv", [P, 2, TILES, 2])
    var_eps = sb("var_eps", [P, 2, TILES])
    rstd = sb("rstd", [P, 2, TILES])
    xn = sb("xn", [P, 2, TILES, D])
    spare = sb("spare", [P, 1])
    scaled = sb("scaled", [P, 2, TILES])
    squares = sb("squares", [P, 2, TILES])
    sums_eps = sb("sums_eps", [P, 2, TILES])
    rms = sb("rms", [P, 2, TILES])
    un = sb("un", [P, 2, TILES, D])
    unT = sb("unT", [P, 2, SEQ])
    drive = sb("drive", [S, 2, SEQ])
    states = sb("states", [S + 1, 2, SEQ])

    p_x = [pb(f"p_x{h}", [P, SEQ]) for h in range(2)]
    p_u = [pb(f"p_u{h}", [P, SEQ]) for h in range(2)]
    p_proj = [pb(f"p_proj{h}", [P, SEQ]) for h in range(2)]
    p_y = [pb(f"p_y{h}", [P, SEQ]) for h in range(2)]

    early_in, late_in, u_in = sem("early_in"), sem("late_in"), [sem(f"u_in{h}") for h in range(2)]
    set_up, ones_ready, col_done, sigm, expd, b_ready = sem("set_up"), sem("ones_ready"), sem("col_done"), sem("sigm"), sem("expd"), sem("b_ready")
    hi_split, wo_split, w2_split, w1_ready, folded = sem("hi_split"), sem("wo_split"), sem("w2_split"), sem("w1_ready"), sem("folded")
    u_stat, u_mv, u_var, u_rstd = sem("u_stat"), sem("u_mv"), sem("u_var"), sem("u_rstd")
    xn_ready, scaled_done, squares_done, sums_ready, rms_ready = (
        sem("xn_ready"), sem("scaled_done"), sem("squares_done"), sem("sums_ready"), sem("rms_ready"))
    un_ready, xn_turned, un_turned = sem("un_ready"), sem("xn_turned"), sem("un_turned")
    x_copied, un_copied, projected, driven = sem("x_copied"), sem("un_copied"), sem("projected"), sem("driven")
    scanned, y_done, acc_ready, acc_out = sem("scanned"), sem("y_done"), sem("acc_ready"), sem("acc_out")

    vec = lambda a: a.rearrange("(a b) -> a b", b=1)
    early = [(w["ident"][:, :], i["ident"]), (dt_a[:, 0:1], vec(i["dt"])), (dt_a[:, 1:2], vec(i["A"])),
             (b_raw[:, :], i["Bmat"]), (norm_w[:, :], vec(i["norm_w"])), (c_d[0:S, :], i["C"]),
             (c_d[S:S + 1, :], i["D"].rearrange("(a b) -> a b", a=1))]
    late = [(rot_raw[:, 0], i["rot_cos"]), (rot_raw[:, 1], i["rot_sin"]),
            (q_mask_raw[:, :, :], i["q_mask"]), (k_mask_raw[:, :, :], i["k_mask"]), (sel_raw[:, :, :], i["sel"])]
    for l in range(LAYERS):
        late += [(scales[:, l, 0, :], i["q_scale"][l:l + 1, :].partition_broadcast(P)),
                 (scales[:, l, 1, :], i["k_scale"][l:l + 1, :].partition_broadcast(P)),
                 (ln_g[:, l:l + 1], vec(i["ln_g"][l])), (ln_b[:, l:l + 1], vec(i["ln_b"][l])),
                 (w["b2"][:, l:l + 1], vec(i["b2"][l])),
                 (wo_raw[:, l], i["wo"][l].rearrange("(c p) d -> p c d", p=P)),
                 (wqkv_raw[:, l], i["wqkv"][l]), (w1_raw[:, l], i["w1"][l])]
        for j in range(HB):
            late.append((w2_raw[0:HROWS[j], l, j], i["w2"][l, HM * j:HM * j + HROWS[j], :]))
            for a in range(2):
                at = a * HID + HM * j
                late.append((b1_raw[0:HROWS[j], l, HB * a + j:HB * a + j + 1], vec(i["b1"][l, at:at + HROWS[j]])))

    def iterations(eng, step, last, after_two=None, before_drain=None):
        for n in range(NB // 2):
            step(n, n % 2)
            if n == 1 and after_two:
                after_two()
        with eng.Fori(NB // 4, NB // 2) as p:
            for half in range(2):
                step(2 * p + half, half)
        for n in range(NB, NB + last + 1):
            step(n, n % 2)
            if n == NB and before_drain:
                before_drain()

    def there(b):
        return not isinstance(b, int) or 0 <= b < NB

    def scale_tables(eng, l):
        for t in range(TILES):
            eng.tensor_tensor(w["cos"][:, l, t], rot_raw[:, 0, t], scales[:, l], ALU.mult)
            for h in range(2):
                eng.tensor_tensor(w["sin"][:, l, t, :, 32 * h:32 * h + 32], rot_raw[:, 1, t, :, 32 * h:32 * h + 32],
                                  scales[:, l, :, 32 - 32 * h:64 - 32 * h], ALU.mult)

    def tile_of_u(b, t):
        return u[:, bass.ds(b * SEQ + t * D, D)]

    block = ctx.enter_context(nc.Block())

    @block.sync
    def _(sp):
        def load(b, half):
            wait(sp, u_in[half], 16 * (b // 2))
            sp.dma_start(u[:, b * SEQ:(b + 1) * SEQ].rearrange("p (t d) -> p t d", t=TILES), u_tok[b]).then_inc(u_in[half], 16)

        for b in range(2):
            load(b, b)
        for dst, src in early:
            sp.dma_start(dst, src).then_inc(early_in, 16)
        for b in range(2, 6):
            load(b, b % 2)
        for dst, src in late:
            sp.dma_start(dst, src).then_inc(late_in, 16)
        with sp.Fori(3, NB // 2) as p:
            for half in range(2):
                sp.wait_ge(u_in[half], 16 * p)
                sp.dma_start(u[:, bass.ds((2 * p + half) * SEQ, SEQ)].rearrange("p (t d) -> p t d", t=TILES),
                             u_tok[2 * p + half]).then_inc(u_in[half], 16)

    @block.gpsimd
    def _(pool):
        def step(n, half):
            if there(n - 1):
                b, h = n - 1, 1 - half
                pool.wait_ge(sums_ready, b + 1)
                wait(pool, un_ready, b - 1)
                nc.gpsimd.tensor_tensor(rms[:, h], sums_eps[:, h], w["minus_half"][:, 0:TILES], ALU.pow).then_inc(rms_ready, 1)
            if there(n):
                pool.wait_ge(u_var, n + 1)
                wait(pool, xn_ready, n - 1)
                nc.gpsimd.tensor_tensor(rstd[:, half], var_eps[:, half], w["minus_half"][:, 0:TILES], ALU.pow).then_inc(u_rstd, 1)

        def constants():
            pool.wait_ge(late_in, 16 * len(late))
            for l in range(LAYERS):
                nc.gpsimd.tensor_scalar(w1_scaled[:, l], w1_raw[:, l], ln_g[:, l:l + 1], None, ALU.mult).then_inc(w1_ready, 1)
            scale_tables(nc.gpsimd, 1)
            pool.wait_ge(wo_split, 1)
            nc.gpsimd.tensor_tensor(w["wo_lo"][:, :], wo_raw[:, :], w["wo_hi"][:, :].bitcast(F32), ALU.subtract)
            pool.wait_ge(w2_split, HB)
            for j in range(HB):
                rows = slice(0, HROWS[j])
                nc.gpsimd.tensor_tensor(w["w2_lo"][rows, :, j], w2_raw[rows, :, j], w["w2_hi"][rows, :, j].bitcast(F32), ALU.subtract)
            for l in range(LAYERS):
                pool.wait_ge(hi_split, 2 * l + 2)
                nc.gpsimd.tensor_tensor(w["w1_lo"][:, l], w1_scaled[:, l], w["w1_hi"][:, l].bitcast(F32), ALU.subtract)

        pool.memset(w["minus_half"][:, :], -0.5).then_inc(set_up, 1)
        pool.wait_ge(set_up, 1)
        iterations(pool, step, 0, before_drain=constants)

    @block.vector
    def _(dve):
        def set_up_decay():
            count = [0]

            def chained(instruction):
                instruction.then_inc(col_done, 1)
                count[0] += 1
                dve.wait_ge(col_done, count[0])

            dve.wait_ge(early_in, 16 * len(early))
            nc.vector.tensor_scalar(b_mat[:, :], b_raw[:, :], norm_w[:, 0:1], None, ALU.mult).then_inc(b_ready, 1)
            dve.wait_ge(sigm, 1)
            chained(nc.vector.tensor_scalar(col[:, 1:2], col[:, 0:1], 1.0, None, ALU.add))
            chained(nc.vector.reciprocal(col[:, 2:3], col[:, 1:2]))
            chained(nc.vector.tensor_scalar(col[:, 3:4], dt_a[:, 1:2], -1.0, None, ALU.mult))
            chained(nc.vector.tensor_tensor(col[:, 4:5], col[:, 3:4], dt_a[:, 1:2], ALU.min))
            chained(nc.vector.tensor_tensor(col[:, 5:6], col[:, 4:5], col[:, 2:3], ALU.mult))
            chained(nc.vector.tensor_scalar(col[:, 6:7], col[:, 5:6], -0.35, None, ALU.max))
            chained(nc.vector.memset(col[:, 8:9], 1.0 / 9))
            for order in range(8, -1, -1):
                at = 8 + (9 - order)
                chained(nc.vector.tensor_scalar(col[:, at:at + 1], col[:, at - 1:at], col[:, 6:7], 1.0, ALU.mult, ALU.add))
                if order > 1:
                    chained(nc.vector.tensor_scalar(col[:, at:at + 1], col[:, at:at + 1], 1.0 / order, None, ALU.mult))
            chained(nc.vector.tensor_scalar(col[:, 18:19], col[:, 5:6], -0.35, None, ALU.is_gt))
            dve.wait_ge(expd, 1)
            chained(nc.vector.tensor_tensor(col[:, 19:20], col[:, 17:18], col[:, 7:8], ALU.subtract))
            chained(nc.vector.tensor_tensor(col[:, 20:21], col[:, 19:20], col[:, 18:19], ALU.mult))
            chained(nc.vector.tensor_tensor(col[:, 21:22], col[:, 20:21], col[:, 7:8], ALU.add))
            chained(nc.vector.memset(decay[:, :], 1.0))
            chained(nc.vector.tensor_scalar(decay[:, :], decay[:, :], col[:, 21:22], None, ALU.mult))

        def step(n, half):
            if there(n - 4):
                b = n - 4
                dve.wait_ge(driven, b + 1)
                wait(dve, y_done, b - 1)
                nc.vector.tensor_tensor_scan(states[0:S, half], decay[:, :], drive[:, half], 0.0,
                                             ALU.mult, ALU.add).then_inc(scanned, 1)
            if there(n - 5):
                b = n - 5
                at = bass.ds(b * SEQ, SEQ)
                dve.wait_ge(y_done, b + 1)
                nc.vector.tensor_tensor(u[:, at], p_y[1 - half][:, :], u[:, at], ALU.add).then_inc(acc_ready, 1)
            if there(n):
                dve.wait_ge(u_in[half], 16 * (n // 2) + 16 if isinstance(n, int) else 8 * (n - half) + 16)
                for t in range(TILES):
                    last = nc.vector.bn_stats(stats[:, half, t], tile_of_u(n, t))
                last.then_inc(u_stat, 1)
            if there(n - 1):
                b, h = n - 1, 1 - half
                dve.wait_ge(u_rstd, b + 1)
                nc.vector.tensor_tensor(scaled[:, h], mv[:, h, :, 1], rstd[:, h], ALU.mult).then_inc(scaled_done, 1)
                wait(dve, un_ready, b - 1)
                for t in range(TILES):
                    last = nc.vector.tensor_scalar(xn[:, h, t], tile_of_u(b, t), mv[:, h, t, 0:1],
                                                   rstd[:, h, t:t + 1], ALU.subtract, ALU.mult)
                last.then_inc(xn_ready, 1)
                dve.wait_ge(scaled_done, b + 1)
                nc.vector.tensor_tensor(squares[:, h], scaled[:, h], rstd[:, h], ALU.mult).then_inc(squares_done, 1)
            if there(n):
                dve.wait_ge(u_stat, n + 1)
                nc.vector.memset(spare[:, :], 0.0)
                for t in range(TILES):
                    last = nc.vector.bn_aggr(mv[:, half, t], stats[:, half, t])
                last.then_inc(u_mv, 1)
            if there(n - 1):
                dve.wait_ge(squares_done, n)
                nc.vector.tensor_scalar(sums_eps[:, 1 - half], squares[:, 1 - half], 1e-6, None, ALU.add).then_inc(sums_ready, 1)
            if there(n):
                dve.wait_ge(u_mv, n + 1)
                nc.vector.tensor_scalar(var_eps[:, half], mv[:, half, :, 1], 1e-5, None, ALU.add).then_inc(u_var, 1)

        def constants():
            dve.wait_ge(late_in, 16 * len(late))
            nc.vector.tensor_copy(w["ident_b"][:, :], w["ident"][:, :])
            nc.vector.tensor_copy(w["q_mask"][:, :, :], q_mask_raw[:, :, :])
            nc.vector.tensor_copy(w["k_mask"][:, :, :], k_mask_raw[:, :, :])
            nc.vector.tensor_copy(w["sel"][:, :, :], sel_raw[:, :, :])
            scale_tables(nc.vector, 0)
            for l in range(LAYERS):
                dve.wait_ge(hi_split, 2 * l + 1)
                nc.vector.tensor_tensor(w["wqkv_lo"][:, l], wqkv_raw[:, l], w["wqkv_hi"][:, l].bitcast(F32), ALU.subtract)

        nc.vector.memset(states[S:S + 1, :, :], 1.0).then_inc(ones_ready, 1)
        iterations(dve, step, LAG, set_up_decay, constants)

        dve.wait_ge(folded, 1)
        for l in range(LAYERS):
            for j in range(HB):
                for a in range(2):
                    at = HB * a + j
                    nc.vector.tensor_tensor(w["b1"][0:HROWS[j], l, at:at + 1], p_x[0][0:HROWS[j], 6 * l + at:6 * l + at + 1],
                                            b1_raw[0:HROWS[j], l, at:at + 1], ALU.add)

    @block.scalar
    def _(act):
        act.wait_ge(early_in, 16 * len(early))
        nc.scalar.activation(col[:, 0:1], dt_a[:, 0:1], ACT.Exp, scale=-1.0).then_inc(sigm, 1)
        act.wait_ge(col_done, 5)
        nc.scalar.activation(col[:, 7:8], col[:, 5:6], ACT.Exp).then_inc(expd, 1)

        def step(n, half):
            if there(n - 2):
                b = n - 2
                act.wait_ge(rms_ready, b + 1)
                act.wait_ge(xn_ready, b + 1)
                wait(act, un_turned, b - 1)
                for t in range(TILES):
                    last = nc.scalar.activation(un[:, half, t], xn[:, half, t], ACT.Copy, scale=rms[:, half, t:t + 1])
                last.then_inc(un_ready, 1)
            if there(n - 3):
                b, h = n - 3, 1 - half
                act.wait_ge(projected, b + 1)
                wait(act, scanned, b - 1)
                nc.scalar.activation(drive[:, h], p_proj[h][0:S, :], ACT.Copy, scale=col[:, 2:3]).then_inc(driven, 1)
            if there(n - 1):
                b, h = n - 1, 1 - half
                act.wait_ge(xn_turned, b + 1)
                nc.scalar.copy(w["xT"][:, bass.ds(b * SEQ, SEQ)], p_x[h][:, :]).then_inc(x_copied, 1)
            if there(n - 2):
                b = n - 2
                act.wait_ge(un_turned, b + 1)
                wait(act, projected, b - 1)
                nc.scalar.copy(unT[:, half], p_u[half][:, :]).then_inc(un_copied, 1)
            if there(n - 5):
                b = n - 5
                act.wait_ge(acc_ready, b + 1)
                act.dma_start(acc_tok[b], u[:, bass.ds(b * SEQ, SEQ)].rearrange("p (t d) -> p t d", t=TILES)).then_inc(acc_out, 16)

        def constants():
            act.wait_ge(late_in, 16 * len(late))
            nc.scalar.copy(w["wo_hi"][:, :], wo_raw[:, :]).then_inc(wo_split, 1)
            for j in range(HB):
                nc.scalar.copy(w["w2_hi"][0:HROWS[j], :, j], w2_raw[0:HROWS[j], :, j]).then_inc(w2_split, 1)
            for l in range(LAYERS):
                nc.scalar.copy(w["wqkv_hi"][:, l], wqkv_raw[:, l]).then_inc(hi_split, 1)
                act.wait_ge(w1_ready, l + 1)
                nc.scalar.copy(w["w1_hi"][:, l], w1_scaled[:, l]).then_inc(hi_split, 1)

        iterations(act, step, LAG, before_drain=constants)
        act.wait_ge(acc_out, 16 * NB)

    @block.tensor
    def _(pe):
        def step(n, half):
            if there(n - 4):
                b = n - 4
                pe.wait_ge(scanned, b + 1)
                wait(pe, acc_ready, b - 1)
                for t in range(TILES):
                    last = nc.tensor.matmul(p_y[half][:, t * P:(t + 1) * P], states[:, half, t * P:(t + 1) * P], c_d[:, :],
                                            start=True, stop=True)
                last.then_inc(y_done, 1)
            if there(n - 3):
                b, h = n - 3, 1 - half
                if isinstance(b, int) and b == 0:
                    pe.wait_ge(b_ready, 1)
                pe.wait_ge(un_copied, b + 1)
                wait(pe, driven, b - 1)
                nc.tensor.matmul(p_proj[h][0:S, :], b_mat[:, :], unT[:, h], start=True, stop=True).then_inc(projected, 1)
            if there(n - 1):
                b, h = n - 1, 1 - half
                pe.wait_ge(xn_ready, b + 1)
                wait(pe, x_copied, b - 1)
                for t in range(TILES):
                    last = nc.tensor.transpose(p_x[h][:, t * P:(t + 1) * P], xn[:, h, t], w["ident"][:, :])
                last.then_inc(xn_turned, 1)
            if there(n - 2):
                b = n - 2
                pe.wait_ge(un_ready, b + 1)
                wait(pe, un_copied, b - 1)
                for t in range(TILES):
                    last = nc.tensor.transpose(p_u[half][:, t * P:(t + 1) * P], un[:, half, t], w["ident"][:, :])
                last.then_inc(un_turned, 1)

        pe.wait_ge(early_in, 16 * len(early))
        pe.wait_ge(ones_ready, 1)
        iterations(pe, step, 4)
        pe.wait_ge(late_in, 16 * len(late))
        pe.wait_ge(x_copied, NB)
        for l in range(LAYERS):
            for j in range(HB):
                for a in range(2):
                    at = a * HID + HM * j
                    last = nc.tensor.matmul(p_x[0][0:HROWS[j], 6 * l + HB * a + j:6 * l + HB * a + j + 1],
                                            w1_raw[:, l, at:at + HROWS[j]], ln_b[:, l:l + 1], start=True, stop=True)
        last.then_inc(folded, 1)


def layer_steps(nc, ctx, acc_tok, out_tok, w):
    def sb(name, shape, dt=F32):
        return ctx.enter_context(nc.sbuf_tensor(name, shape, dt))

    def pb(name, shape, dt=F32):
        return ctx.enter_context(nc.psum_tensor(name, shape, dt))

    def sem(name):
        return ctx.enter_context(nc.semaphore(name))

    xT = w["xT"]
    h_hi = sb("h_hi", [P, SEQ], F32R)
    h_lo = sb("h_lo", [P, SEQ], F32R)
    sq = sb("sq", [P, 2 * HEADS, DH])
    rot_a = sb("rot_a", [P, 2, HEADS, DH])
    rot_b = sb("rot_b", [P, 2, HEADS, DH])
    qk_n = sb("qk_n", [P, 2, 2 * HEADS, DH])
    ss = sb("ss", [P, 2 * HEADS])
    ss_clip = sb("ss_clip", [P, 2 * HEADS])
    rn = sb("rn", [P, 2 * HEADS])
    qT = sb("qT", [P, PAIRS, P])
    qT_hi = sb("qT_hi", [P, PAIRS, P], F32R)
    kT = sb("kT", [P, PAIRS, WIN + SEQ])
    kT_hi = sb("kT_hi", [P, PAIRS, WIN + SEQ], F32R)
    v_own = sb("v_own", [P, TILES, HEADS, DH + 1])
    v_mix = sb("v_mix", [P, TILES, HEADS, DH + 1])
    mx = sb("mx", [P, 2, PAIRS])
    mx_b = sb("mx_b", [P, 2, 2 * PAIRS], BF16)
    mxT = sb("mxT", [2 * HEADS, P], BF16)
    probs = [sb(f"probs{g}", [P, PAIRS, 2, WIN]) for g in range(2)]
    rden = sb("rden", [P, 2, PAIRS])
    o_tok = sb("o_tok", [P, PAIRS, 2, DH])
    oT = sb("oT", [P, 2, PAIRS, P])
    oT_hi = sb("oT_hi", [P, PAIRS, SEQ], F32R)
    oT_lo = sb("oT_lo", [P, PAIRS, SEQ], F32R)
    x1 = sb("x1", [P, SEQ])
    h2 = sb("h2", [P, SEQ + 1])
    stats = sb("stats_f", [P, TILES, 6])
    mv = sb("mv_f", [P, TILES, 2])
    var_eps = sb("var_eps_f", [P, TILES])
    rs = sb("rs", [P, TILES])
    h2_tok = sb("h2_tok", [P, TILES, P])
    hn = sb("hn", [P, TILES, P])
    hn_hi = sb("hn_hi", [P, SEQ], F32R)
    hn_lo = sb("hn_lo", [P, SEQ], F32R)
    gate = [h2_tok[0:HM, :, :].rearrange("p t d -> p (t d)"), hn[0:HM, :, :].rearrange("p t d -> p (t d)")]
    gated = sb("gated", [HM, 2, SEQ])
    g_hi = sb("g_hi", [HM, 2, SEQ], F32R)
    g_lo = sb("g_lo", [HM, 2, SEQ], F32R)
    gated_hi = [g_hi[:, 0], g_hi[:, 1], hn_hi[0:HM, :]]
    gated_lo = [g_lo[:, 0], g_lo[:, 1], hn_lo[0:HM, :]]
    acc = sb("acc", [P, SEQ])

    p_qk = pb("p_qk", [P, 2, INNER])
    p_v = pb("p_v", [P, 512])
    p_t = pb("p_t", [P, 512])
    p_bank = {bank: pb(f"p_bank{bank}", [P, 512])[:, :] for bank in (4, 5, 6)}
    p_query = [p_bank[bank][:, 0:2 * (P + WIN)] for bank in (4, 5, 6, 4)]
    p_st = [p_bank[bank].rearrange("p (j q) -> p j q", j=PAIRS) for bank in (6, 5)]
    p_o = pb("p_o", [P, 512])
    p_oh = p_o[:, 0:PAIRS * (DH + 1)].rearrange("p (j d) -> p j d", j=PAIRS)
    p_mx = p_o[0:2 * HEADS, 384:448].bitcast(BF16)

    zeroed = sem("zeroed")
    h_hi_ready, h_lo_ready = sem("h_hi_ready"), sem("h_lo_ready")
    qk_done, v_done, sq_done, v_copied = sem("qk_done"), sem("v_done"), sem("sq_done"), sem("v_copied")
    rot_done, ss_sum, ss_ready, rn_ready = sem("rot_done"), sem("ss_sum"), sem("ss_ready"), sem("rn_ready")
    added, qkn_ready, q_turned, k_turned = sem("added"), sem("qkn_ready"), sem("q_turned"), sem("k_turned")
    qT_ready, q_hi_ready, kT_ready = sem("qT_ready"), sem("q_hi_ready"), sem("kT_ready")
    v_mixed = [sem(f"v_mixed{t}") for t in range(TILES)]
    s_done, max_done, mx_hi, mx_ready = sem("s_done"), sem("max_done"), sem("mx_hi"), sem("mx_ready")
    mx_turned, mxT_ready, st_done, p_ready = sem("mx_turned"), sem("mxT_ready"), sem("st_done"), sem("p_ready")
    pv_done, den_ready, o_ready, o_turned, oT_ready = sem("pv_done"), sem("den_ready"), sem("o_ready"), sem("o_turned"), sem("oT_ready")
    o_hi_ready, o_lo_ready, h2_late_ready = sem("o_hi_ready"), sem("o_lo_ready"), sem("h2_late_ready")
    wo_done, x1_ready, h2_ready, h2_turned, h2_copied = sem("wo_done"), sem("x1_ready"), sem("h2_ready"), sem("h2_turned"), sem("h2_copied")
    stat_done, mv_done, var_ready, rs_ready = sem("stat_done"), sem("mv_done"), sem("var_ready"), sem("rs_ready")
    hn_ready, hn_turned, hn_hi_ready, hn_lo_ready = sem("hn_ready"), sem("hn_turned"), sem("hn_hi_ready"), sem("hn_lo_ready")
    gate_done, up_done, gelu_ready, gated_ready = sem("gate_done"), sem("up_done"), sem("gelu_ready"), sem("gated_ready")
    gated_hi_ready, gated_lo_ready, third_lo_ready = sem("gated_hi_ready"), sem("gated_lo_ready"), sem("third_lo_ready")
    w2_done, x2_ready, x2_turned, ffn_done = sem("w2_done"), sem("x2_ready"), sem("x2_turned"), sem("ffn_done")
    acc_in, result_ready, out_stored = sem("acc_in"), sem("result_ready"), sem("out_stored")

    def run(eng, step):
        step(0, 0, None, None)
        step(1, 0, 0, None)
        with eng.Fori(2, NB) as s:
            step(s, 0, 0, 0)
        step(NB, 1, 0, 0)
        step(NB + 1, 1, 1, 0)
        with eng.Fori(NB + 2, STEPS) as s:
            step(s, 1, 1, 1)
        step(STEPS, None, 1, 1)
        step(STEPS + 1, None, None, 1)

    def slots(s, layer, before, tail):
        new, old = layer is not None, before is not None
        for t in range(TILES):
            yield (t, 4 * s + t, new, (new if t >= 2 else old), (new if t >= 3 else old),
                   old and t == 3, tail is not None and t < 3)

    block = ctx.enter_context(nc.Block())

    @block.sync
    def _(sp):
        def step(s, layer, before, tail):
            for t, n, new, scored, weighed, begun, ended in slots(s, layer, before, tail):
                if new:
                    sp.wait_ge(v_copied, n + 1)
                    sp.dma_start(v_mix[0:WIN, t, :, 0:DH], v_own[0:WIN, t, :, 0:DH]).then_inc(v_mixed[t], 16)
                    if t < TILES - 1:
                        wait(sp, pv_done, 2 * (n - 3) + 2)
                        sp.dma_start(v_mix[WIN:P, t + 1, :, 0:DH], v_own[WIN:P, t, :, 0:DH]).then_inc(v_mixed[t], 16)
                if tail == 1 and t == 3 and not (isinstance(s, int) and s == STEPS + 1):
                    b = s - NB - 1
                    sp.wait_ge(out_stored, 16 * b)
                    sp.dma_start(acc[:, :].rearrange("p (t d) -> p t d", t=TILES), acc_tok[b]).then_inc(acc_in, 16)

        sp.dma_start(acc[:, :].rearrange("p (t d) -> p t d", t=TILES), acc_tok[0]).then_inc(acc_in, 16)
        run(sp, step)

    @block.gpsimd
    def _(pool):
        def rest_of_o(r, v):
            at = slice(P * v, P * (v + 1))
            pool.wait_ge(o_hi_ready, r + 1)
            nc.gpsimd.tensor_tensor(oT_lo[:, :, at], oT[:, v % 2], oT_hi[:, :, at].bitcast(F32), ALU.subtract).then_inc(o_lo_ready, 1)

        def rest_of_gated(k, j):
            r = HROWS[j]
            pool.wait_ge(gated_hi_ready, HB * (k - 1) + j + 1)
            nc.gpsimd.tensor_tensor(gated_lo[j][0:r], gated[0:r, j % 2], gated_hi[j][0:r].bitcast(F32),
                                    ALU.subtract).then_inc(gated_lo_ready, 1)

        def step(s, layer, before, tail):
            for t, n, new, scored, weighed, begun, ended in slots(s, layer, before, tail):
                if ended and t == 0:
                    pool.wait_ge(var_ready, s - 1)
                    nc.gpsimd.tensor_tensor(rs[:, :], var_eps[:, :], w["minus_half"][:, 0:TILES], ALU.pow).then_inc(rs_ready, 1)
                if ended and t == 2:
                    rest_of_gated(s - 1, 1)
                if weighed and not begun:
                    rest_of_o(n - 3, (t - 3) % TILES)
                if new:
                    pool.wait_ge(ss_ready, n + 1)
                    wait(pool, qkn_ready, n)
                    nc.gpsimd.tensor_tensor(rn[:, :], ss_clip[:, :], w["minus_half"][:, :], ALU.pow).then_inc(rn_ready, 1)
                    pool.wait_ge(rot_done, 2 * n + 2)
                    wait(pool, k_turned, n - 1)
                    nc.gpsimd.tensor_tensor(qk_n[:, t % 2].rearrange("p h d -> p (h d)"),
                                            rot_a[:, :, :, :].rearrange("p a h d -> p (a h d)"),
                                            rot_b[:, :, :, :].rearrange("p a h d -> p (a h d)"), ALU.add).then_inc(added, 1)
                    pool.wait_ge(rn_ready, n + 1)
                    pool.wait_ge(added, n + 1)
                    nc.gpsimd.tensor_tensor(qk_n[:, t % 2], qk_n[:, t % 2],
                                            rn[:, :].unsqueeze(2).to_broadcast([P, 2 * HEADS, DH]), ALU.mult).then_inc(qkn_ready, 1)
                if ended and t == 1:
                    rest_of_gated(s - 1, 0)
                if weighed and begun:
                    rest_of_o(n - 3, 0)

        run(pool, step)

    @block.scalar
    def _(act):
        def split_rounded(s):
            at = (s % NB) * SEQ
            wait(act, qk_done, 8 * s)
            nc.scalar.copy(h_hi[0:WIN, :], xT[0:WIN, bass.ds(at, SEQ)])
            nc.scalar.copy(h_hi[WIN:P, 1:SEQ], xT[WIN:P, bass.ds(at, SEQ - 1)]).then_inc(h_hi_ready, 1)

        def copy_o(r, v):
            act.wait_ge(o_turned, r + 1)
            wait(act, o_lo_ready, r - 1)
            nc.scalar.copy(oT[:, v % 2], p_t[:, :].rearrange("p (j c) -> p j c", j=PAIRS)).then_inc(oT_ready, 1)

        def round_o(r, v):
            act.wait_ge(oT_ready, r + 1)
            nc.scalar.copy(oT_hi[:, :, P * v:P * (v + 1)], oT[:, v % 2]).then_inc(o_hi_ready, 1)

        def square(n, part):
            act.wait_ge(qk_done, 2 * n + part + 1)
            nc.scalar.activation(sq[:, HEADS * part:HEADS * (part + 1), :].rearrange("p h d -> p (h d)"),
                                 p_qk[:, part, :], ACT.Square).then_inc(sq_done, 1)

        def gelu(k, layer, j):
            r = HROWS[j]
            act.wait_ge(gate_done, HB * (k - 1) + j + 1)
            nc.scalar.activation(gate[j % 2][0:r], p_v[0:r, :], ACT.Gelu,
                                 bias=w["b1"][0:r, layer, HB + j:HB + j + 1]).then_inc(gelu_ready, 1)

        def round_gated(k, j):
            r = HROWS[j]
            act.wait_ge(gated_ready, HB * (k - 1) + j + 1)
            wait(act, w2_done, k - 1)
            nc.scalar.copy(gated_hi[j][0:r], gated[0:r, j % 2]).then_inc(gated_hi_ready, 1)

        def exp(m, g):
            act.wait_ge(st_done, 2 * m + g + 1)
            wait(act, pv_done, 2 * m + g - 1)
            nc.scalar.activation(probs[g][:, :, :, :].rearrange("p j w q -> p (j w q)"),
                                 p_st[g].rearrange("p j q -> p (j q)"), ACT.Exp, scale=QK_SCALE).then_inc(p_ready, 1)

        def step(s, layer, before, tail):
            for t, n, new, scored, weighed, begun, ended in slots(s, layer, before, tail):
                m, u = n - 2, (t - 2) % TILES
                if scored:
                    act.wait_ge(k_turned, m + 1)
                    tile = slice(WIN + P * u, WIN + P * (u + 1))
                    k_blocks = p_bank[4].rearrange("p (j c) -> p j c", j=PAIRS)
                    nc.scalar.copy(kT_hi[:, :, tile], k_blocks)
                    nc.scalar.copy(kT[:, :, tile], k_blocks).then_inc(kT_ready, 1)
                if new:
                    act.wait_ge(v_done, n + 1)
                    nc.scalar.copy(v_own[:, t, :, 0:DH], p_v[:, :].rearrange("p (h d) -> p h d", h=HEADS)).then_inc(v_copied, 1)
                if ended and t == 1:
                    gelu(s - 1, tail, 0)
                if ended and t == 2:
                    gelu(s - 1, tail, 2)
                if weighed and not begun and ended and t >= 1:
                    copy_o(n - 3, (t - 3) % TILES)
                if ended and t == 2:
                    round_gated(s - 1, 1)
                if new:
                    wait(act, ss_ready, n)
                    square(n, 0)
                if weighed and not begun and not (ended and t >= 1):
                    copy_o(n - 3, (t - 3) % TILES)
                if new:
                    square(n, 1)
                if weighed and not begun:
                    round_o(n - 3, (t - 3) % TILES)
                if ended and t == 1:
                    round_gated(s - 1, 0)
                if ended and t == 2:
                    round_gated(s - 1, 2)
                if new and t == 3 and not (isinstance(s, int) and s + 1 == STEPS):
                    split_rounded(s + 1)
                if begun:
                    act.wait_ge(x1_ready, s)
                    nc.scalar.copy(h2[0:WIN, 0:SEQ], x1[0:WIN, :]).then_inc(h2_ready, 1)
                    if weighed:
                        copy_o(n - 3, 0)
                elif ended and t == 1:
                    gelu(s - 1, tail, 1)
                if scored:
                    exp(m, 0)
                if begun:
                    act.wait_ge(h2_turned, s)
                    nc.scalar.copy(h2_tok[:, :, :].rearrange("p t d -> p (t d)"), p_v[:, :]).then_inc(h2_copied, 1)
                    if weighed:
                        round_o(n - 3, 0)
                if scored:
                    exp(m, 1)
                if ended and t == 0:
                    act.wait_ge(hn_turned, s - 1)
                    nc.scalar.copy(hn_hi[:, :], p_bank[6]).then_inc(hn_hi_ready, 1)
                if tail == 1 and t == 3:
                    b = s - NB - 2
                    act.wait_ge(result_ready, b + 1)
                    act.dma_start(out_tok[b], acc[:, :].rearrange("p (t d) -> p t d", t=TILES)).then_inc(out_stored, 16)

        act.wait_ge(zeroed, 8)
        split_rounded(0)
        run(act, step)
        act.wait_ge(out_stored, 16 * NB)

    @block.vector
    def _(dve):
        def split_rest(s):
            at = (s % NB) * SEQ
            dve.wait_ge(h_hi_ready, s + 1)
            nc.vector.tensor_tensor(h_lo[0:WIN, :], xT[0:WIN, bass.ds(at, SEQ)], h_hi[0:WIN, :].bitcast(F32), ALU.subtract)
            nc.vector.tensor_tensor(h_lo[WIN:P, 1:SEQ], xT[WIN:P, bass.ds(at, SEQ - 1)],
                                    h_hi[WIN:P, 1:SEQ].bitcast(F32), ALU.subtract).then_inc(h_lo_ready, 1)

        def weighed_mean(m, g):
            dve.wait_ge(pv_done, 2 * m + g + 1)
            nc.vector.reciprocal(rden[:, g, :], p_oh[:, :, DH]).then_inc(den_ready, 1)
            dve.wait_ge(den_ready, 2 * m + g + 1)
            wait(dve, o_turned, m)
            nc.vector.tensor_tensor(o_tok[:, :, g, :], p_oh[:, :, 0:DH],
                                    rden[:, g, :].unsqueeze(2).to_broadcast([P, PAIRS, DH]), ALU.mult).then_inc(o_ready, 1)

        def maxima(m, unit):
            g, b = unit // 2, unit % 2
            dve.wait_ge(s_done, 4 * m + unit + 1)
            nc.vector.tensor_reduce(mx[:, g, 2 * b:2 * b + 2],
                                    p_query[unit].rearrange("p (b c) -> p b c", b=2), AX.X, ALU.max).then_inc(max_done, 1)

        def rotate(layer, t, n, part):
            dve.wait_ge(sq_done, 2 * n + part + 1)
            heads = p_qk[:, part, :].rearrange("p (h d) -> p h d", h=HEADS)
            for half in range(2):
                to, other = slice(32 * half, 32 * half + 32), slice(32 - 32 * half, 64 - 32 * half)
                nc.vector.tensor_tensor(rot_b[:, part, :, to], heads[:, :, other],
                                        w["sin"][:, layer, t, part, to].unsqueeze(1).to_broadcast([P, HEADS, 32]), ALU.mult)
            nc.vector.tensor_tensor(rot_a[:, part], heads, w["cos"][:, layer, t, part].unsqueeze(1).to_broadcast([P, HEADS, DH]),
                                    ALU.mult).then_inc(rot_done, 1)

        def gated_values(k, layer, j):
            r = HROWS[j]
            dve.wait_ge(up_done, HB * (k - 1) + j + 1)
            dve.wait_ge(gelu_ready, HB * (k - 1) + j + 1)
            if j == 2:
                dve.wait_ge(gated_lo_ready, 2 * (k - 1) + 1)
            nc.vector.scalar_tensor_tensor(gated[0:r, j % 2], p_t[0:r, :], w["b1"][0:r, layer, j:j + 1], gate[j % 2][0:r],
                                           ALU.add, ALU.mult).then_inc(gated_ready, 1)

        def step(s, layer, before, tail):
            for t, n, new, scored, weighed, begun, ended in slots(s, layer, before, tail):
                m = n - 2
                if scored:
                    dve.wait_ge(q_turned, m + 1)
                    nc.vector.tensor_copy(qT[:, :, :].rearrange("p j c -> p (j c)"), p_t[:, :]).then_inc(qT_ready, 1)
                    dve.wait_ge(qT_ready, m + 1)
                    nc.vector.tensor_copy(qT_hi[:, :, :], qT[:, :, :]).then_inc(q_hi_ready, 1)
                if weighed:
                    weighed_mean(n - 3, 0)
                if tail is not None and t == 1:
                    dve.wait_ge(hn_hi_ready, s - 1)
                    nc.vector.tensor_tensor(hn_lo[:, :], p_bank[6], hn_hi[:, :].bitcast(F32), ALU.subtract).then_inc(hn_lo_ready, 1)
                if tail == 1 and t == 3:
                    b = s - NB - 2
                    dve.wait_ge(x2_turned, b + 1)
                    dve.wait_ge(acc_in, 16 * (b + 1))
                    nc.vector.tensor_tensor(acc[:, :], p_bank[6], acc[:, :], ALU.add).then_inc(result_ready, 1)
                if scored:
                    for unit in range(3):
                        maxima(m, unit)
                if weighed:
                    weighed_mean(n - 3, 1)
                if scored:
                    maxima(m, 3)
                    dve.wait_ge(max_done, 4 * m + 4)
                    wait(dve, mx_turned, m)
                    nc.vector.tensor_copy(mx_b[:, 0, :], mx[:, :, :].rearrange("p g j -> p (g j)")).then_inc(mx_hi, 1)
                    dve.wait_ge(mx_hi, m + 1)
                    nc.vector.tensor_tensor(mx_b[:, 1, :], mx[:, :, :].rearrange("p g j -> p (g j)"), mx_b[:, 0, :],
                                            ALU.subtract).then_inc(mx_ready, 1)
                if ended and t == 0:
                    dve.wait_ge(stat_done, s - 1)
                    nc.vector.memset(var_eps[:, 0:1], 0.0)
                    for c in range(TILES):
                        last = nc.vector.bn_aggr(mv[:, c], stats[:, c])
                    last.then_inc(mv_done, 1)
                    dve.wait_ge(mv_done, s - 1)
                    nc.vector.tensor_scalar(var_eps[:, :], mv[:, :, 1], 1e-5, None, ALU.add).then_inc(var_ready, 1)
                if scored:
                    dve.wait_ge(mx_turned, m + 1)
                    nc.vector.tensor_copy(mxT[:, :], p_mx).then_inc(mxT_ready, 1)
                if ended and t == 2:
                    gated_values(s - 1, tail, 2)
                if new:
                    wait(dve, added, n)
                    rotate(layer, t, n, 0)
                if ended and t == 1:
                    gated_values(s - 1, tail, 0)
                if ended and t == 2:
                    k, r = s - 1, HROWS[2]
                    dve.wait_ge(gated_hi_ready, HB * k)
                    nc.vector.tensor_tensor(gated_lo[2][0:r], gated[0:r, 0], gated_hi[2][0:r].bitcast(F32),
                                            ALU.subtract).then_inc(third_lo_ready, 1)
                if new:
                    dve.wait_ge(sq_done, 2 * n + 2)
                    nc.vector.tensor_reduce(ss[:, :], sq[:, :, :], AX.X, ALU.add).then_inc(ss_sum, 1)
                if ended and t == 0:
                    dve.wait_ge(rs_ready, s - 1)
                    wait(dve, hn_turned, s - 2)
                    for c in range(TILES):
                        last = nc.vector.tensor_scalar(hn[:, c], h2_tok[:, c], mv[:, c, 0:1], rs[:, c:c + 1],
                                                       ALU.subtract, ALU.mult)
                    last.then_inc(hn_ready, 1)
                if begun:
                    x_at = bass.ds((s - 1 - NB * before) * SEQ, SEQ)
                    dve.wait_ge(wo_done, s)
                    nc.vector.tensor_tensor(x1[:, :], p_v[:, :], xT[:, x_at], ALU.add).then_inc(x1_ready, 1)
                if new:
                    dve.wait_ge(ss_sum, n + 1)
                    wait(dve, rn_ready, n)
                    nc.vector.tensor_scalar(ss_clip[:, :], ss[:, :], 1e-24, None, ALU.max).then_inc(ss_ready, 1)
                if begun:
                    dve.wait_ge(x1_ready, s)
                    wait(dve, h2_turned, s - 1)
                    nc.vector.tensor_copy(h2[WIN:P, 1:SEQ + 1], x1[WIN:P, :]).then_inc(h2_late_ready, 1)
                if new:
                    rotate(layer, t, n, 1)
                if ended and t == 1:
                    gated_values(s - 1, tail, 1)
                if new and t == 3 and not (isinstance(s, int) and s + 1 == STEPS):
                    split_rest(s + 1)
                if begun:
                    dve.wait_ge(h2_copied, s)
                    for c in range(TILES):
                        last = nc.vector.bn_stats(stats[:, c], h2_tok[:, c])
                    last.then_inc(stat_done, 1)
                if ended and t == 2:
                    dve.wait_ge(w2_done, s - 1)
                    if tail == 0:
                        nc.vector.scalar_tensor_tensor(xT[:, bass.ds((s - 2) * SEQ, SEQ)], p_v[:, :], w["b2"][:, 0:1], x1[:, :],
                                                       ALU.add, ALU.add).then_inc(ffn_done, 1)
                    else:
                        b = s - NB - 2
                        nc.vector.scalar_tensor_tensor(x1[:, :], p_v[:, :], w["b2"][:, 1:2], x1[:, :],
                                                       ALU.add, ALU.add).then_inc(x2_ready, 1)

        nc.vector.memset(kT[:, :, 0:WIN], 0.0).then_inc(zeroed, 1)
        nc.vector.memset(kT_hi[:, :, 0:WIN].bitcast(F32), 0.0).then_inc(zeroed, 1)
        nc.vector.memset(v_own[:, :, :, DH:DH + 1], 1.0).then_inc(zeroed, 1)
        nc.vector.memset(v_mix[:, :, :, DH:DH + 1], 1.0).then_inc(zeroed, 1)
        nc.vector.memset(v_mix[WIN:P, 0, :, 0:DH], 0.0).then_inc(zeroed, 1)
        nc.vector.memset(h_hi[WIN:P, 0:1].bitcast(F32), 0.0).then_inc(zeroed, 1)
        nc.vector.memset(h_lo[WIN:P, 0:1].bitcast(F32), 0.0).then_inc(zeroed, 1)
        nc.vector.memset(h2[WIN:P, 0:1], 0.0).then_inc(zeroed, 1)
        split_rest(0)
        run(dve, step)

    @block.tensor
    def _(pe):
        def project(s, layer, t, n, parts):
            tok = slice(P * t, P * (t + 1))
            for part in parts:
                dst = [p_qk[:, 0, :], p_qk[:, 1, :], p_v[:, :]][part]
                cols = slice(INNER * part, INNER * (part + 1))
                nc.tensor.matmul(dst, h_hi[:, tok], w["wqkv_lo"][:, layer, cols], start=True, stop=False)
                nc.tensor.matmul(dst, h_lo[:, tok], w["wqkv_hi"][:, layer, cols], start=False, stop=False)
                last = nc.tensor.matmul(dst, h_hi[:, tok], w["wqkv_hi"][:, layer, cols], start=False, stop=True)
            return last

        def project_q(s, layer, t, n):
            wait(pe, rot_done, 2 * n - 1)
            project(s, layer, t, n, (0,)).then_inc(qk_done, 1)

        def project_k(s, layer, t, n):
            wait(pe, rot_done, 2 * n)
            project(s, layer, t, n, (1,)).then_inc(qk_done, 1)

        def project_v(s, layer, t, n, tail):
            if t == 0:
                pe.wait_ge(h_hi_ready, s + 1)
                pe.wait_ge(h_lo_ready, s + 1)
            wait(pe, v_copied, n)
            if tail is not None:
                k = s - 1
                if t == 0:
                    pe.wait_ge(h2_copied, k)
                if t == 2:
                    pe.wait_ge(gelu_ready, HB * (k - 1) + 2)
                if t == 3:
                    wait_tail_read(s, tail)
            project(s, layer, t, n, (2,)).then_inc(v_done, 1)

        def wait_tail_read(s, tail):
            if tail == 0:
                pe.wait_ge(ffn_done, s - 1)
            else:
                pe.wait_ge(x2_ready, s - NB - 1)

        def turn_qk(s, m, t, tail):
            pe.wait_ge(qkn_ready, m + 1)
            wait(pe, oT_ready, m - 1)
            if tail is not None and t == 2:
                pe.wait_ge(gated_ready, HB * (s - 2) + 2)
            if tail is not None and t == 3:
                pe.wait_ge(gated_ready, HB * (s - 1))
            flat = qk_n[:, t % 2].rearrange("p h d -> p (h d)")
            for j in range(PAIRS):
                last = nc.tensor.transpose(p_t[:, P * j:P * (j + 1)], flat[:, P * j:P * (j + 1)], w["ident"][:, :])
            last.then_inc(q_turned, 1)
            wait(pe, max_done, 4 * m)
            for j in range(PAIRS):
                last = nc.tensor.transpose(p_bank[4][:, P * j:P * (j + 1)], flat[:, INNER + P * j:INNER + P * (j + 1)], w["ident"][:, :])
            last.then_inc(k_turned, 1)

        def scores_by_query(s, tail, m, u, units):
            for unit in units:
                g, b = unit // 2, unit % 2
                rows = slice(DH * g, DH * (g + 1))
                if unit == 0:
                    pe.wait_ge(q_hi_ready, m + 1)
                    pe.wait_ge(kT_ready, m + 1)
                if unit == 1:
                    wait(pe, p_ready, 2 * m)
                if unit == 2 and tail is not None and u == 3:
                    pe.wait_ge(hn_lo_ready, s - 1)
                if unit == 2 and tail == 1 and u == 1:
                    pe.wait_ge(result_ready, s - NB - 1)
                if unit == 3:
                    pe.wait_ge(max_done, 4 * m + 1)
                nc.tensor.matmul(p_query[unit].rearrange("p (b c) -> p b c", b=2), w["ident_b"][:, :],
                                 w["q_mask"][:, min(u, 1), :].unsqueeze(1).to_broadcast([P, 2, P + WIN]),
                                 start=True, stop=False, skip_group_check=True)
                for c in range(2):
                    last = nc.tensor.matmul(p_query[unit][:, c * (P + WIN):(c + 1) * (P + WIN)], qT_hi[rows, 2 * b + c, :],
                                            kT_hi[rows, 2 * b + c, P * u:P * (u + 1) + WIN], start=False, stop=True, skip_group_check=True)
                last.then_inc(s_done, 1)

        def scores_by_key(m, u, g):
            rows = slice(DH * g, DH * (g + 1))
            if g == 0:
                pe.wait_ge(mxT_ready, m + 1)
            dst = p_st[g]
            nc.tensor.matmul(dst, w["ident_b"][:, :], w["k_mask"][:, min(u, 1), :].unsqueeze(1).to_broadcast([P, PAIRS, P]),
                             start=True, stop=False, skip_group_check=True)
            for j in range(PAIRS):
                nc.tensor.matmul(dst[:, j, :], w["sel"][:, 2 * j + g, :], mxT[:, :], start=False, stop=False, skip_group_check=True)
            even, before, odd = WIN + P * u, P * u, 2 * WIN + P * u
            for j in range(PAIRS):
                nc.tensor.matmul(dst[0:WIN, j, :], kT[rows, j, even:even + WIN], qT[rows, j, :],
                                 start=False, stop=True, skip_group_check=True)
                nc.tensor.matmul(dst[WIN:P, j, 0:WIN], kT[rows, j, before:before + WIN], qT[rows, j, 0:WIN],
                                 start=False, stop=True, skip_group_check=True)
                last = nc.tensor.matmul(dst[WIN:P, j, WIN:P], kT[rows, j, odd:odd + WIN], qT[rows, j, WIN:P],
                                        start=False, stop=True, skip_group_check=True)
            last.then_inc(st_done, 1)

        def weigh(s, m, u, g):
            if g == 0:
                pe.wait_ge(v_mixed[u], (32 if u < TILES - 1 else 16) * (s + 1 if u == 0 else s))
            pe.wait_ge(p_ready, 2 * m + g + 1)
            wait(pe, o_ready, 2 * m + g)
            for j in range(PAIRS):
                for win, v in ((0, v_mix), (1, v_own)):
                    last = nc.tensor.matmul(p_oh[WIN * win:WIN * (win + 1), j, :], probs[g][:, j, win, :], v[:, u, 2 * j + g, :],
                                            start=True, stop=True, skip_group_check=True)
            last.then_inc(pv_done, 1)

        def hidden(k, layer, j, a):
            r = HROWS[j]
            dst, done = (p_v, gate_done) if a else (p_t, up_done)
            at = a * HID + HM * j
            cols = slice(at, at + r)
            nc.tensor.matmul(dst[0:r, :], w["w1_lo"][:, layer, cols], hn_hi[:, :], start=True, stop=False)
            nc.tensor.matmul(dst[0:r, :], w["w1_hi"][:, layer, cols], hn_lo[:, :], start=False, stop=False)
            nc.tensor.matmul(dst[0:r, :], w["w1_hi"][:, layer, cols], hn_hi[:, :], start=False, stop=True).then_inc(done, 1)

        def turn(dst, src, done):
            for c in range(TILES):
                last = nc.tensor.transpose(dst[:, P * c:P * (c + 1)], src(c), w["ident"][:, :])
            last.then_inc(done, 1)

        def step(s, layer, before, tail):
            for t, n, new, scored, weighed, begun, ended in slots(s, layer, before, tail):
                u, v, k = (t - 2) % TILES, (t - 3) % TILES, s - 1
                if scored:
                    turn_qk(s, n - 2, t, tail)
                if t == 3 and tail == 1:
                    pe.wait_ge(x2_ready, s - NB - 1)
                    if scored:
                        pe.wait_ge(p_ready, 2 * (n - 3) + 1)
                    turn(p_bank[6], lambda c: x1[:, P * c:P * (c + 1)], x2_turned)
                if weighed:
                    weigh(s, n - 3, v, 0)
                if new:
                    project_v(s, layer, t, n, tail)
                if scored:
                    scores_by_query(s, tail, n - 2, u, (0, 1, 2))
                if weighed:
                    weigh(s, n - 3, v, 1)
                if scored:
                    scores_by_query(s, tail, n - 2, u, (3,))
                if ended and t >= 1:
                    if new:
                        pe.wait_ge(v_copied, n + 1)
                    pe.wait_ge(*((hn_lo_ready, k) if t == 1 else (gelu_ready, HB * (k - 1) + 2)))
                    hidden(k, tail, 0 if t == 1 else 2, 1)
                if weighed and ended and t >= 1:
                    turn_o(n, scored)
                if new:
                    project_q(s, layer, t, n)
                if weighed and not begun and not (ended and t >= 1):
                    turn_o(n, scored)
                if new and begun:
                    project_k(s, layer, t, n)
                if scored and not begun:
                    turn_maxima(n, weighed)
                if new and not begun:
                    project_k(s, layer, t, n)
                if ended and t >= 1:
                    if weighed:
                        pe.wait_ge(oT_ready, n - 2)
                    elif t == 2:
                        pe.wait_ge(gated_ready, HB * (k - 1) + 2)
                    hidden(k, tail, 0 if t == 1 else 2, 0)
                if begun:
                    pe.wait_ge(o_lo_ready, 4 * s)
                    if new:
                        pe.wait_ge(v_copied, n + 1)
                    elif tail is not None:
                        wait_tail_read(s, tail)
                    for c in range(PAIRS):
                        nc.tensor.matmul(p_v[:, :], w["wo_lo"][:, before, c, :], oT_hi[:, c, :], start=(c == 0), stop=False)
                        nc.tensor.matmul(p_v[:, :], w["wo_hi"][:, before, c, :], oT_lo[:, c, :], start=False, stop=False)
                        last = nc.tensor.matmul(p_v[:, :], w["wo_hi"][:, before, c, :], oT_hi[:, c, :], start=False, stop=(c == PAIRS - 1))
                        if c == 0 and scored:
                            turn_maxima(n, weighed)
                    last.then_inc(wo_done, 1)
                    if weighed:
                        turn_o(n, scored)
                if scored:
                    scores_by_key(n - 2, u, 0)
                if begun:
                    pe.wait_ge(h2_ready, s)
                    pe.wait_ge(h2_late_ready, s)
                    turn(p_v, lambda c: h2[:, P * c:P * (c + 1)], h2_turned)
                if ended and t == 1:
                    pe.wait_ge(gelu_ready, HB * (k - 1) + 1)
                    hidden(k, tail, 1, 1)
                    pe.wait_ge(gated_ready, HB * (k - 1) + 1)
                    hidden(k, tail, 1, 0)
                if ended and t == 2:
                    pe.wait_ge(gelu_ready, HB * k)
                    for j in range(2):
                        weigh_hidden(k, tail, j)
                if scored:
                    scores_by_key(n - 2, u, 1)
                if ended and t == 2:
                    weigh_hidden(k, tail, 2)
                if ended and t == 0:
                    pe.wait_ge(hn_ready, k)
                    if scored:
                        pe.wait_ge(p_ready, 2 * (n - 2) + 1)
                    turn(p_bank[6], lambda c: hn[:, c], hn_turned)

        def weigh_hidden(k, layer, j):
            r = slice(0, HROWS[j])
            pe.wait_ge(*((gated_lo_ready, 2 * (k - 1) + j + 1) if j < 2 else (third_lo_ready, k)))
            nc.tensor.matmul(p_v[:, :], w["w2_hi"][r, layer, j, :], gated_lo[j][r], start=(j == 0), stop=False)
            nc.tensor.matmul(p_v[:, :], w["w2_lo"][r, layer, j, :], gated_hi[j][r], start=False, stop=False)
            last = nc.tensor.matmul(p_v[:, :], w["w2_hi"][r, layer, j, :], gated_hi[j][r], start=False, stop=(j == HB - 1))
            if j == HB - 1:
                last.then_inc(w2_done, 1)

        def turn_maxima(n, weighed):
            if weighed:
                pe.wait_ge(o_ready, 2 * (n - 3) + 2)
            pe.wait_ge(mx_ready, n - 1)
            nc.tensor.transpose(p_mx, mx_b[:, :, :].rearrange("p a h -> p (a h)"), w["ident_b"][:, :]).then_inc(mx_turned, 1)

        def turn_o(n, scored):
            pe.wait_ge(o_ready, 2 * (n - 3) + 2)
            if scored:
                pe.wait_ge(qT_ready, n - 1)
            wait(pe, oT_ready, n - 3)
            turn(p_t, lambda c: o_tok[:, c, :, :].rearrange("p g d -> p (g d)"), o_turned)

        run(pe, step)


_INPUTS = {"u": "L0_attn_u", "dt": "L0_attn_dt", "A": "L0_attn_A", "Bmat": "L0_attn_Bmat", "C": "L0_attn_C",
           "D": "L0_attn_D", "norm_w": "L0_attn_norm_w", "wqkv": "L0_ffn_wqkv", "q_scale": "L0_ffn_q_scale",
           "k_scale": "L0_ffn_k_scale", "wo": "L0_ffn_wo", "ln_g": "L0_ffn_ln_g", "ln_b": "L0_ffn_ln_b",
           "w1": "L0_ffn_w1", "b1": "L0_ffn_b1", "w2": "L0_ffn_w2", "b2": "L0_ffn_b2"}


def kernel(**inputs):
    import concourse.bacc as bacc
    from concourse.bass_utils import run_bass_kernel_spmd

    nc = bacc.Bacc("TRN2", target_bir_lowering=False, num_devices=1)
    rot_cos, rot_sin = rotary_tables()
    q_mask, k_mask = masks()
    arrays = {name: np.ascontiguousarray(inputs[full]) for name, full in _INPUTS.items()}
    arrays |= {"rot_cos": rot_cos, "rot_sin": rot_sin, "q_mask": q_mask, "k_mask": k_mask,
               "sel": selectors(), "ident": np.eye(P, dtype=np.float32)}
    aps = {name: nc.dram_tensor(f"in_{name}", a.shape, F32, kind="ExternalInput").ap() for name, a in arrays.items()}
    out = nc.dram_tensor("out", (NB, SEQ, D), F32, kind="ExternalOutput").ap()
    acc = nc.dram_tensor("first_sums", (NB, SEQ, D), F32, kind="Internal").ap()
    build(nc, aps, out, acc)
    r = run_bass_kernel_spmd(nc, [{f"in_{name}": a for name, a in arrays.items()}], core_ids=[0])
    return r.results[0]["out"]
```
